# Optimizing a Trainium2 kernel written in Bass

```python
import numpy as np
import jax
import jax.numpy as jnp

def _softmax(x, axis=-1):
    return jax.nn.softmax(x, axis=axis)

def _gelu(x):
    return jax.nn.gelu(x, approximate=True)

def _silu(x):
    return jax.nn.silu(x)

def _sigmoid(x):
    return jax.nn.sigmoid(x)

def _layernorm(x, axis=-1, eps=1e-05):
    m = jnp.mean(x, axis=axis, keepdims=True)
    v = jnp.var(x, axis=axis, keepdims=True)
    return (x - m) / jnp.sqrt(v + eps)

def _scatter_add(tgt, idx, src, axis=0):
    return tgt.at[idx].add(src)

def _segment_sum(src, seg, n):
    return jax.ops.segment_sum(src, seg, n)
kernel_name = 'mk_conv_preact_d1_conv_nhwc768_r2_8650c2'

def setup_inputs(seed: int=0):
    np.random.seed(seed)
    _w = jnp.asarray

    def _rec_inputs():
        import jax
        import jax.numpy as jnp
        _gk = jax.random.key(seed)
        x = -0.0002221 + 1 * jax.random.normal(jax.random.fold_in(_gk, 1), (8, 32, 32, 384), jnp.float32)
        return x
    x = _rec_inputs()

    def _L0_conv_setup():
        import jax, jax.numpy as jnp
        import numpy as np
        DIM = 384
        NUM_BLOCKS = 4
        BLOCK = DIM // NUM_BLOCKS
        SCALE = 0.02

        def _block_mul(t, w):
            return jnp.einsum('...bd,bdk->...bk', t, w)
        key = jax.random.key(seed)
        ks = jax.random.split(key, 7)
        x = jax.random.normal(ks[0], (8, 32, 32, DIM), dtype=jnp.float32)
        w1 = SCALE * jax.random.normal(ks[1], (2, NUM_BLOCKS, BLOCK, BLOCK), dtype=jnp.float32)
        b1 = SCALE * jax.random.normal(ks[2], (2, NUM_BLOCKS, BLOCK), dtype=jnp.float32)
        w2 = SCALE * jax.random.normal(ks[3], (2, NUM_BLOCKS, BLOCK, BLOCK), dtype=jnp.float32)
        b2 = SCALE * jax.random.normal(ks[4], (2, NUM_BLOCKS, BLOCK), dtype=jnp.float32)
        lim = 1.0 / np.sqrt(DIM)
        bias_w = jax.random.uniform(ks[5], (DIM, DIM), minval=-lim, maxval=lim, dtype=jnp.float32)
        bias_b = jax.random.uniform(ks[6], (DIM,), minval=-lim, maxval=lim, dtype=jnp.float32)
        return {'x': x, 'w1': w1, 'b1': b1, 'w2': w2, 'b2': b2, 'bias_w': bias_w, 'bias_b': bias_b}
    _L0_conv_all = _L0_conv_setup()
    _L0_conv_in = {k: v for k, v in _L0_conv_all.items() if k in ('w1', 'b1', 'w2', 'b2', 'bias_w', 'bias_b')}
    del _L0_conv_all
    return {'x': x, 'L0_conv_w1': _L0_conv_in['w1'], 'L0_conv_b1': _L0_conv_in['b1'], 'L0_conv_w2': _L0_conv_in['w2'], 'L0_conv_b2': _L0_conv_in['b2'], 'L0_conv_bias_w': _L0_conv_in['bias_w'], 'L0_conv_bias_b': _L0_conv_in['bias_b']}

def reference(x, L0_conv_w1, L0_conv_b1, L0_conv_w2, L0_conv_b2, L0_conv_bias_w, L0_conv_bias_b):
    import jax
    import jax.numpy as jnp

    def _L0_conv_ref(x, w1, b1, w2, b2, bias_w, bias_b):
        import jax, jax.numpy as jnp
        import numpy as np
        DIM = 384
        NUM_BLOCKS = 4
        BLOCK = DIM // NUM_BLOCKS
        SCALE = 0.02

        def _block_mul(t, w):
            return jnp.einsum('...bd,bdk->...bk', t, w)
        B, H, W, C = x.shape
        nb = w1.shape[1]
        bs = C // nb
        bias = x @ bias_w.T + bias_b
        xb = x.reshape(B, H, W, nb, bs)
        xf = jnp.fft.rfftn(xb, axes=(1, 2), norm='ortho')
        xr, xi = (xf.real, xf.imag)
        r1 = jax.nn.relu(_block_mul(xr, w1[0]) - _block_mul(xi, w1[1]) + b1[0])
        i1 = jax.nn.relu(_block_mul(xr, w1[1]) + _block_mul(xi, w1[0]) + b1[1])
        r2 = _block_mul(r1, w2[0]) - _block_mul(i1, w2[1]) + b2[0]
        i2 = _block_mul(r2, w2[1]) + _block_mul(i1, w2[0]) + b2[1]
        xc = jax.lax.complex(r2, i2)
        out = jnp.fft.irfftn(xc, s=(H, W), axes=(1, 2), norm='ortho')
        out = out.reshape(B, H, W, C)
        return out + bias

    def _gn(v, G=32, eps=1e-05):
        B_, H_, W_, C_ = v.shape
        g = v.reshape(B_, H_, W_, G, C_ // G)
        m = jnp.mean(g, axis=(1, 2, 4), keepdims=True)
        s = jnp.var(g, axis=(1, 2, 4), keepdims=True)
        return ((g - m) / jnp.sqrt(s + eps)).reshape(v.shape)

    def _ln_c(v, eps=1e-06):
        m = jnp.mean(v, axis=-1, keepdims=True)
        s = jnp.var(v, axis=-1, keepdims=True)
        return (v - m) / jnp.sqrt(s + eps)

    def _ln_t(v, eps=1e-05):
        m = jnp.mean(v, axis=-1, keepdims=True)
        s = jnp.var(v, axis=-1, keepdims=True)
        return (v - m) / jnp.sqrt(s + eps)

    def _to_tokens(v):
        B_, H_, W_, C_ = v.shape
        return v.reshape(B_, H_ * W_, C_)

    def _from_tokens(t, like):
        return t.reshape(like.shape)
    x = x + _L0_conv_ref(_gn(x), L0_conv_w1, L0_conv_b1, L0_conv_w2, L0_conv_b2, L0_conv_bias_w, L0_conv_bias_b)
    return x

_drawn_inputs = setup_inputs


def setup_inputs(seed=0):
    import zlib

    import numpy as np

    out = dict(_drawn_inputs(seed))
    spreads = {}
    factors = {'L0_conv_b1': 8.0}
    for name, (base, spread) in spreads.items():
        noise = np.random.default_rng([zlib.crc32(name.encode()), seed]).standard_normal(out[name].shape)
        drawn = base * np.exp(spread * noise) if base else spread * noise
        out[name] = jnp.asarray(drawn.astype(out[name].dtype))
    for name, factor in factors.items():
        out[name] = (out[name] * factor).astype(out[name].dtype)
    return out
```

```python
import numpy as np
import concourse.bass as bass
from concourse import mybir
from contextlib import ExitStack

BATCHES, SIDE, CH = 8, 32, 384
BLOCKS, BC = 4, 96
GROUP = 12
TILES = 8
KT = 4
PIX = SIDE * SIDE
GN_EPS = 1e-5
ROOT = float(np.sqrt(SIDE))


def fourier_tables():
    w = np.arange(SIDE)
    width = np.zeros((2, 4, SIDE, 2, 2, 2, 16))
    for kind in range(2):
        for j in range(2):
            first = kind == 0 and j == 0
            for kw in range(17):
                c = np.cos(2 * np.pi * kw * w / SIDE) / ROOT
                s = -np.sin(2 * np.pi * kw * w / SIDE) / ROOT
                t = width[kind, 2 * j:2 * j + 2]
                half = np.sqrt(0.5)
                if kw in (0, 16):
                    x = kw // 16
                    if first:
                        t[0, :, 0, j, x, 15] = c
                        t[1, :, 1, j, x, 15] = c
                    else:
                        t[:, :, 0, j, x, 15] = half * c
                        t[0, :, 1, j, x, 15] = -half * c
                        t[1, :, 1, j, x, 15] = half * c
                elif first:
                    for e in range(2):
                        t[e, :, 0, j, e, kw - 1] = c
                        t[e, :, 1, j, e, kw - 1] = s
                else:
                    t[:, :, 0, j, 0, kw - 1] = half * c
                    t[:, :, 1, j, 0, kw - 1] = half * s
                    for m, sign in ((0, 1), (1, -1)):
                        t[m, :, 0, j, 1, kw - 1] = sign * half * s
                        t[m, :, 1, j, 1, kw - 1] = -sign * half * c
    kh = np.arange(SIDE)
    height = np.zeros((SIDE, 16, 2))
    height[:, 0, 0] = 1
    height[:, 0, 1] = (-1.0) ** kh
    for q in range(1, 16):
        height[:, q, 0] = np.sqrt(2) * np.cos(2 * np.pi * kh * q / SIDE)
        height[:, q, 1] = np.sqrt(2) * np.sin(2 * np.pi * kh * q / SIDE)
    height /= ROOT
    hgt = np.zeros((2, TILES, 2, 2, 4, 4, SIDE))
    rows = height.reshape(SIDE, TILES, 2, 2)
    for slot in range(4):
        for kind in range(2 if slot < 3 else 1):
            hgt[kind, :, :, :, slot, slot] = rows.transpose(1, 2, 3, 0)
    xf = np.zeros((2, 2, TILES, 2, 2, 2, 2, SIDE))
    xi = np.zeros((2, 2, SIDE, 2, 66))
    xia = np.zeros((2, 2, SIDE, 2, TILES, 2, 2))
    xib = np.zeros_like(xia)
    for t in range(TILES):
        for j in range(2):
            q = 2 * t + j
            for x in range(2):
                for part in range(2):
                    xf[part, 0, t, j, x, part, x] = height[:, q, 0]
                    xia[part, x, :, part, t, j, x] = height[:, q, 0]
                    if q == 0:
                        xf[part, 1, t, j, x, part, x] = height[:, 0, 1]
                        xi[part, x, :, part, 64 + x] = height[:, 0, 1]
                    else:
                        xf[part, 1, t, j, x, 1 - part, x] = height[:, q, 1] * (1 if part == 0 else -1)
                        xib[part, x, :, part, t, j, x] = height[:, q, 1]
    xi[..., 0:32] = xia.reshape(2, 2, SIDE, 2, 32)
    xi[..., 32:64] = xib.reshape(2, 2, SIDE, 2, 32)
    back = width.copy()
    back[..., 0:15] *= 2
    width = width.reshape(2, 128, 2, 64)
    back = back.reshape(2, 128, 2, 64)
    inv = np.zeros((3, 128, 128))
    for n, (kind, odd) in enumerate(((0, 0), (1, 0), (1, 1))):
        r, i = back[kind, :, 0].T, back[kind, :, 1].T
        inv[n] = np.concatenate([i, r] if odd else [r, i])
    const = np.zeros((2, TILES, 2, 2))
    for t in range(TILES):
        got = width[0 if t == 0 else 1].sum(0).reshape(2, 2, 2, 16)[..., 15]
        const[:, t] = np.where(np.abs(got) < 1e-9, 0, got)
    return width, hgt.reshape(2, 128, 128), xf.reshape(128, 128), xi.reshape(128, 132), inv, const.reshape(64)


def group_tables():
    own = np.zeros((128, 128))
    block3 = np.zeros((BC, 4, 128))
    for a in range(128):
        for b in range(128):
            if a % 4 < 3 and b % 4 < 3 and (a // 4 * 3 + a % 4) // GROUP == (b // 4 * 3 + b % 4) // GROUP:
                own[a, b] = 1 / GROUP
    for n in range(BC):
        for m in range(BC):
            if n // GROUP == m // GROUP:
                block3[n, m // 32, 4 * (m % 32) + 3] = 1 / GROUP
                block3[n, 3, m] = 1 / GROUP
    return own, block3


TAB = {}
TABW = 0
for _name, _wide in (("width", 256), ("height", 256), ("xf", 128), ("xi", 132), ("heightT", 256), ("inv", 384),
                     ("own", 128), ("block3", 512), ("const", 64), ("rowscale", 1)):
    TAB[_name] = (TABW, TABW + _wide)
    TABW += _wide


def constants():
    width, hgt, xf, xi, inv, const = fourier_tables()
    own, block3 = group_tables()
    tab = np.zeros((128, TABW))

    def put(name, a):
        tab[:a.shape[0], TAB[name][0]:TAB[name][1]] = a.reshape(a.shape[0], -1)

    put("width", width.reshape(2, 128, 128).transpose(1, 0, 2))
    put("height", hgt.transpose(1, 0, 2))
    put("xf", xf)
    put("xi", xi)
    put("heightT", np.concatenate([hgt[0].T, hgt[1].T.reshape(128, 32, 4)[:, :, 0:3].reshape(128, 96), np.zeros((128, 32))], axis=1))
    put("inv", inv.transpose(1, 0, 2))
    put("own", own)
    put("block3", block3)
    put("const", np.broadcast_to(const, (128, 64)))
    tab[96:99, TAB["rowscale"][0]] = [ROOT, ROOT, 8.0]
    mark = np.zeros((3, TILES, 2, 2, 16))
    mark[0, 0, 0, 0, :] = 1
    mark[0, 0, 0, 1, 15] = 1
    mark_a = mark.copy()
    mark_a[1, 0, 0, 0, 15] = 1
    mark_a[2, :, :, 0, 15] = 1
    mark_a[2, 0, 0, 0, 15] = 0
    mark_b = mark.copy()
    mark_b[0, 0, 0, :, 15] = 0
    extra = np.zeros((3, 32))
    extra[1, 15] = 1
    marks = np.concatenate([mark_a.reshape(3, 512), mark_b.reshape(3, 512), extra], axis=1)
    return tab.astype(np.float32), marks.astype(np.float32)


def spectral_block_kernel(nc, x, w1, b1, b1h, w2, w2t, b2, bias_wt, bias_b, tab_d, marks_d, out):
    f32 = mybir.dt.float32
    ALU = mybir.AluOpType
    ACT = mybir.ActivationFunctionType
    AX = mybir.AxisListType
    ctx = ExitStack()
    with ctx:
        def sb(name, shape, dt=f32):
            return ctx.enter_context(nc.sbuf_tensor(name, shape, dt))

        def sem(name):
            return ctx.enter_context(nc.semaphore(name))

        x_sb = [sb(f"x_sb{p}", [128, TILES, CH]) for p in range(2)]
        o_sb = sb("o_sb", [128, TILES, CH])
        y = [sb(f"y{p}", [128, KT, 2, 512]) for p in range(2)]
        z = sb("z", [128, 9, CH])
        r = sb("r", [128, 9, CH])
        rhoA = sb("rhoA", [128, BLOCKS, 2, 512])
        rhoB = sb("rhoB", [128, BLOCKS, 2, 512])
        rhoX = sb("rhoX", [128, BLOCKS, 2, 32])
        g = sb("g", [128, TILES, CH])
        tab = sb("tab", [128, TABW])
        w1R = sb("w1R", [128, BLOCKS, 2, BC])
        w1I = sb("w1I", [128, BLOCKS, 2, BC])
        biasw = sb("biasw", [128, 3, CH])
        w2s = sb("w2s", [128, BLOCKS, 4, BC])
        w2raw = sb("w2raw", [128, BLOCKS, 2, BC])
        w2T = sb("w2T", [BC, BLOCKS, 2, BC + 3])
        b1s = sb("b1s", [128, 3, CH])
        sumsq = sb("sumsq", [128, KT])
        mc = sb("mc", [128, KT])
        xs1 = sb("xs1", [128, KT, 64])
        xs2 = sb("xs2", [128, KT, 64])
        sX = sb("sX", [128, KT])
        mg = sb("mg", [128, KT])
        dev = sb("dev", [128, KT])
        qv = sb("qv", [128, KT])
        var = sb("var", [128, KT])
        std_t = sb("std_t", [128, KT])
        rstd = sb("rstd", [128, KT])
        nt = sb("nt", [128, KT])
        junk = sb("junk", [128, 960])

        banks = [ctx.enter_context(nc.psum_tensor(f"bank{i}", [128, 512], f32)) for i in range(8)]
        y_bank = banks[0:2]
        b_bank = banks[2:5]
        c_bank = banks[5:8]

        x_loaded = [[sem(f"x_loaded{p}{h}") for h in range(2)] for p in range(2)]
        consts_in = sem("consts_in")
        weights_in = sem("weights_in")
        padded_in = sem("padded_in")
        zeroed = sem("zeroed")
        weights_ready = sem("weights_ready")
        w2_prod = sem("w2_prod")
        y_prod = sem("y_prod")
        y_raw = sem("y_raw")
        y_sq = sem("y_sq")
        mean_prod = sem("mean_prod")
        var_prod = sem("var_prod")
        dve_step = sem("dve_step")
        std_ready = sem("std_ready")
        y_norm = sem("y_norm")
        z_prod = sem("z_prod")
        z_ready = sem("z_ready")
        spec_prod = sem("spec_prod")
        spec_sum = sem("spec_sum")
        r_ready = sem("r_ready")
        rho_prod = sem("rho_prod")
        rho_ready = sem("rho_ready")
        rhoB_ready = sem("rhoB_ready")
        g_prod = sem("g_prod")
        gr_ready = sem("gr_ready")
        gi_ready = sem("gi_ready")
        o_prod = sem("o_prod")
        o_ready = sem("o_ready")
        stored = [sem(f"stored{h}") for h in range(2)]

        NSTEP = 20

        def T(name, n=128, rows=128):
            a = tab[0:rows, TAB[name][0]:TAB[name][1]]
            return a

        width = T("width").rearrange("k (a m) -> k a m", a=2)
        height = T("height").rearrange("k (a m) -> k a m", a=2)
        heightT = T("heightT")
        xf, xi = T("xf"), T("xi")
        inv = T("inv").rearrange("k (a m) -> k a m", a=3)
        own = T("own")
        block3 = T("block3", rows=BC).rearrange("k (a m) -> k a m", a=4)
        const = T("const")
        rowscale = T("rowscale")

        def weight_loads():
            for q in range(3):
                yield biasw[q:128:4, :, :], bias_wt[0:288, :].rearrange("(b i q) n -> q i b n", q=3, b=3)[q]
            yield biasw[3:128:4, :, :], bias_wt[288:384, :].rearrange("(b i) n -> i b n", b=3)
            for ri in range(2):
                yield w2raw[0:BC, :, ri, :], w2[ri].rearrange("b k n -> k b n")
                yield w2T[:, :, ri, 0:BC], w2t[ri].rearrange("b k n -> k b n")
            yield b1s[:, 0:2, :], b1h.rearrange("(o h) n -> o h n", o=1).to_broadcast([128, 2, CH])
            for ri in range(2):
                yield b1s[64 * ri:64 * ri + 64, 2, :], b1[ri].rearrange("(o b) n -> o (b n)", o=1).to_broadcast([64, CH])
            for blk in range(BLOCKS):
                for dst, lo, n in ((rhoA, 0, 512), (rhoB, 512, 512), (rhoX, 1024, 32)):
                    yield dst[BC:BC + 3, blk, 0, 0:n], marks_d[:, lo:lo + n]

        def padded_loads():
            for q in range(3):
                for ri in range(2):
                    yield w1R[q:128:4, 0:3, ri, :], w1[ri, 0:3].rearrange("b (i q) n -> q i b n", q=3)[q]
            yield w1R[0:BC, 3, :, :], w1[:, 3, :, :].rearrange("a k n -> k a n")
            for ri in range(2):
                yield w2raw[BC:BC + 1, :, ri, :], b2[ri].rearrange("(o b) n -> o b n", o=1)
            for row in range(2):
                yield w2raw[BC + 1 + row:BC + 2 + row, :, 0, :], bias_b.rearrange("(o b n) -> o b n", o=1, b=BLOCKS)
            for blk in range(BLOCKS):
                yield w2T[:, blk, 0, BC:BC + 1], b2[0, blk, :].rearrange("(n o) -> n o", o=1)

        N_WEIGHT = len(list(weight_loads()))
        N_PADDED = len(list(padded_loads()))
        N_ZERO = 8
        N_READY = 9
        block = ctx.enter_context(nc.Block())

        @block.sync
        def _(sp):
            def load(b, p):
                for h in range(2):
                    sp.dma_start(x_sb[p][:, 4 * h:4 * h + 4, :].rearrange("p t c -> p (t c)"),
                                 x[b, :, h * 4 * CH:(h + 1) * 4 * CH]).then_inc(x_loaded[p][h], 16)

            sp.dma_start(tab[:, :], tab_d).then_inc(consts_in, 16)
            load(0, 0)
            for dst, src in weight_loads():
                sp.dma_start(dst, src).then_inc(weights_in, 16)
            load(1, 1)
            sp.wait_ge(zeroed, N_ZERO)
            with nc.allow_non_contiguous_dma(reason="one column of 96 per block"):
                for dst, src in padded_loads():
                    sp.dma_start(dst, src).then_inc(padded_in, 16)

            def store(b):
                for h in range(2):
                    sp.wait_ge(o_ready, 8 * b + 8 + 4 * h + 4)
                    sp.dma_start(out[b, :, h * 4 * CH:(h + 1) * 4 * CH],
                                 o_sb[:, 4 * h:4 * h + 4, :].rearrange("p t c -> p (t c)")).then_inc(stored[h], 16)

            with sp.Fori(0, BATCHES - 3, 2) as b:
                for p in range(2):
                    store(b + p)
                    load(b + p + 2, p)
            for p in range(2):
                store(BATCHES - 2 + p)
            for h in range(2):
                sp.wait_ge(stored[h], 16 * BATCHES + 16)

        @block.tensor
        def _(pe):
            def mm(o, lhsT, rhs, start, stop, **kw):
                return nc.tensor.matmul(o, lhsT, rhs, start=start, stop=stop, **kw)

            def p1(b, p, first=False):
                for ct in range(KT):
                    rows = 128 if ct < 3 else BC
                    for h in range(2):
                        m = 2 * ct + h
                        if m >= 2:
                            pe.wait_ge(y_raw, 8 * b + m - 1)
                        elif not first:
                            pe.wait_ge(y_raw, 8 * b + m - 1)
                            if m == 0:
                                pe.wait_ge(dve_step, NSTEP * (b - 1) + 13)
                        if ct == 0:
                            pe.wait_ge(x_loaded[p][h], (b - p) * 8 + 16)
                        for i in range(4):
                            t = 4 * h + i
                            src = x_sb[p][:, t, 128 * ct:128 * ct + 128] if ct < 3 else x_sb[p][:, t, 3:CH:4]
                            last = mm(y_bank[h][0:rows, 128 * i:128 * i + 128], src, width[:, 0 if t == 0 else 1, :], True, True)
                        last.then_inc(y_prod, 1)

            def group_mean(src, at):
                mm(y_bank[0][:, at + 3:at + 4], block3[:, 3, :], src[0:BC, 3:4], True, True)
                mm(y_bank[0][:, at:at + 3], own, src[:, 0:3], True, False)
                for ct in range(3):
                    last = mm(y_bank[0][:, at + ct:at + ct + 1], block3[:, ct, :], src[0:BC, 3:4], False, ct == 2)
                return last

            def mean(b):
                pe.wait_ge(y_raw, 8 * b + 8)
                pe.wait_ge(dve_step, NSTEP * b + 3)
                group_mean(mc, 0).then_inc(mean_prod, 1)

            def variance(b):
                pe.wait_ge(dve_step, NSTEP * b + 12)
                group_mean(qv, 8).then_inc(var_prod, 1)

            def c1(b, p):
                pe.wait_ge(y_norm, 4 * b + 4)
                for u in range(9):
                    if u < 3:
                        pe.wait_ge(o_ready, 8 * b + (7, 8, 6)[u])
                    else:
                        pe.wait_ge(z_ready, 9 * b + u - 2)
                    bank = b_bank[u % 3]
                    if u < 8:
                        t, half = u // 2, u % 2
                        for k in range(2):
                            blk = 2 * half + k
                            K = 128 if blk < 3 else BC
                            o = bank[:, 192 * k:192 * k + 192]
                            mm(o, y[p][0:K, blk, 0, t:512:4], w1R[0:K, blk, :, :].rearrange("k a n -> k (a n)"), True, False)
                            last = mm(o, y[p][0:K, blk, 1, t:512:4], w1I[0:K, blk, :, :].rearrange("k a n -> k (a n)"), False, True)
                    else:
                        for part in range(2):
                            for blk in range(BLOCKS):
                                K = 128 if blk < 3 else BC
                                ys = y[p][0:K, blk, :, :].rearrange("k a n -> k (a n)")[:, 15:1024:16]
                                last = mm(bank[64 * part:64 * part + 64, 96 * blk:96 * blk + 96], ys, w1R[0:K, blk, part, :], True, True)
                    last.then_inc(z_prod, 1)

            def p3(b):
                for u in range(9):
                    if u < 3:
                        if u == 1:
                            pe.wait_ge(gi_ready, 8 * b + 8)
                        elif u == 0:
                            pe.wait_ge(gr_ready, 8 * b + 8)
                        else:
                            pe.wait_ge(gi_ready, 8 * b + 6)
                    else:
                        pe.wait_ge(spec_sum, 9 * b + u - 2)
                    pe.wait_ge(z_ready, 9 * b + u + 1)
                    bank = c_bank[u % 3]
                    if u < 6:
                        last = mm(bank[:, 0:CH], height[:, 0, :], z[:, u, :], True, True)
                    elif u < 8:
                        last = mm(bank[0:96, 0:CH], height[:, 1, 0:96], z[:, u, :], True, True)
                    else:
                        last = mm(bank[:, 0:CH], xf, z[:, u, :], True, True)
                    last.then_inc(spec_prod, 1)

            def p4(b):
                for j in range(10):
                    if j < 3:
                        pe.wait_ge(z_ready, 9 * b + 7 + j)
                    else:
                        pe.wait_ge(rho_ready, 10 * b + j - 2)
                    pe.wait_ge(r_ready, 9 * b + min(j, 8) + 1)
                    bank = b_bank[j % 3]
                    if j < 8:
                        K = 128 if j < 6 else 96
                        n = 128 if j < 6 else 96
                        tabT = heightT[0:K, 0:128] if j < 6 else heightT[0:K, 128:224]
                        for c in range(4):
                            last = mm(bank[0:BC, n * c:n * c + n], r[0:K, j, BC * c:BC * c + BC], tabT, True, True)
                    else:
                        for c in range(2):
                            blk = 2 * (j - 8) + c
                            last = mm(bank[0:BC, 132 * c:132 * c + 132], r[:, 8, BC * blk:BC * blk + BC], xi, True, True)
                    last.then_inc(rho_prod, 1)

            def c2(b, p, gi):
                q, part = gi // 2, gi % 2
                if gi < 3:
                    pe.wait_ge(spec_sum, 9 * b + 7 + gi)
                elif gi % 2:
                    pe.wait_ge(gr_ready, 8 * b + 8 + (gi - 3) + 2)
                else:
                    pe.wait_ge(gi_ready, 8 * b + 8 + (gi - 4) + 2)
                bank = c_bank[gi % 3]
                lo = 128 * q
                for blk in range(BLOCKS):
                    o = bank[:, 96 * blk:96 * blk + 96]
                    rho = rhoB if part else rhoA
                    s0 = rho[0:BC + 3, blk, 0, lo:lo + 128]
                    s1 = rho[0:BC, blk, 1, lo:lo + 128]
                    mm(o, s0, w2s[0:BC + 3, blk, 2 * part, :], blk == 0, False, skip_group_check=True)
                    mm(o, s1, w2s[0:BC, blk, 2 * part + 1, :], False, False, skip_group_check=True)
                    if gi == 1:
                        o = bank[0:32, 96 * blk:96 * blk + 96]
                        mm(o, rhoX[0:BC + 3, blk, 0, :], w2s[0:BC + 3, blk, 0, :], False, False, skip_group_check=True)
                        mm(o, rhoX[0:BC, blk, 1, :], w2s[0:BC, blk, 1, :], False, False, skip_group_check=True)
                for ct in range(3):
                    ys = y[p][:, ct, part, lo:lo + 128]
                    last = mm(bank[:, 0:CH], ys, biasw[:, ct, :], False, ct == 2, skip_group_check=True)
                last.then_inc(g_prod, 1)

            def p6(b):
                for t in range(TILES):
                    if t >= 3:
                        pe.wait_ge(o_ready, 8 * b + 8 + t - 2)
                    pe.wait_ge(gr_ready, 8 * b + 8 + 2 * (t // 2) + 2)
                    pe.wait_ge(gi_ready, 8 * b + 8 + 2 * (t // 2) + 2)
                    mm(b_bank[t % 3][:, 0:CH], inv[:, 0 if t == 0 else 1 + t % 2, :], g[:, t, :], True, True).then_inc(o_prod, 1)

            def image(b, p, more):
                c1(b, p)
                p3(b)
                if more:
                    p1(b + 1, 1 - p)
                p4(b)
                if more:
                    mean(b + 1)
                pe.wait_ge(rho_ready, 10 * b + 10)
                for gi in range(8):
                    if gi == 1:
                        pe.wait_ge(rhoB_ready, 2 * b + 2)
                    c2(b, p, gi)
                    if gi == 2 and more:
                        variance(b + 1)
                p6(b)

            pe.wait_ge(consts_in, 16)
            p1(0, 0, first=True)
            pe.wait_ge(weights_in, 16 * N_WEIGHT)
            pe.wait_ge(padded_in, 16 * N_PADDED)
            for k in range(2):
                for blk in range(BLOCKS):
                    M = BC + 3 if k == 0 else BC
                    last = mm(b_bank[k][0:M, 96 * blk:96 * blk + 96], w2T[:, blk, k, 0:M], w2raw[0:BC, blk, 1, :], True, True)
                last.then_inc(w2_prod, 1)
            mean(0)
            variance(0)
            pe.wait_ge(weights_ready, N_READY)
            with pe.Fori(0, BATCHES - 3, 2) as b:
                for p in range(2):
                    image(b + p, p, True)
            image(BATCHES - 2, 0, True)
            image(BATCHES - 1, 1, False)

        @block.scalar
        def _(act):
            def y_copy(b, p):
                for ct in range(KT):
                    rows = 128 if ct < 3 else BC
                    for h in range(2):
                        act.wait_ge(y_prod, 8 * b + 2 * ct + h + 1)
                        nc.scalar.activation(y[p][0:rows, ct, :, 256 * h:256 * h + 256].rearrange("k a (t m) -> k t a m", t=4),
                                             y_bank[h][0:rows, :].rearrange("k (t a m) -> k t a m", t=4, a=2), ACT.Copy).then_inc(y_raw, 1)
                    act.wait_ge(y_raw, 8 * b + 2 * ct + 2)
                    nc.scalar.activation(junk[:, :].rearrange("k (a m) -> k a m", m=15),
                                         y[p][:, ct, :, :].rearrange("k a (c m) -> k (a c) m", m=16)[:, :, 0:15],
                                         ACT.Square, accum_out=sumsq[:, ct:ct + 1]).then_inc(y_sq, 1)

            def std(b):
                act.wait_ge(dve_step, NSTEP * b + 13)
                nc.scalar.activation(std_t[:, :], var[:, :], ACT.Sqrt).then_inc(std_ready, 1)

            def image(b, p, more):
                for u in range(9):
                    act.wait_ge(z_prod, 9 * b + u + 1)
                    nc.scalar.activation(z[:, u, :], b_bank[u % 3][:, 0:CH], ACT.Copy).then_inc(z_ready, 1)
                for u in range(9):
                    rows = 96 if u in (6, 7) else 128
                    act.wait_ge(spec_sum, 9 * b + u + 1)
                    nc.scalar.activation(r[0:rows, u, :], r[0:rows, u, :], ACT.Relu).then_inc(r_ready, 1)
                if more:
                    y_copy(b + 1, 1 - p)
                for q in range(4):
                    act.wait_ge(g_prod, 8 * b + 2 * q + 1)
                    bank = c_bank[(2 * q) % 3]
                    nc.scalar.activation(g[0:64, 2 * q, :], bank[0:64, 0:CH], ACT.Copy).then_inc(gr_ready, 1)
                    nc.scalar.activation(g[64:128, 2 * q + 1, :], bank[64:128, 0:CH], ACT.Copy).then_inc(gr_ready, 1)
                    if q == 1 and more:
                        std(b + 1)

            act.wait_ge(zeroed, N_ZERO)
            nc.scalar.activation(std_t[:, :], sumsq[:, :], ACT.Copy).then_inc(gr_ready, 8)
            y_copy(0, 0)
            std(0)
            with act.Fori(0, BATCHES - 3, 2) as b:
                for p in range(2):
                    image(b + p, p, True)
            image(BATCHES - 2, 0, True)
            image(BATCHES - 1, 1, False)

        @block.vector
        def _(dve):
            def stat(b, k):
                dve.wait_ge(dve_step, NSTEP * b + k)

            def step(ins):
                ins.then_inc(dve_step, 1)

            def xcols(p):
                return y[p][:, :, :, :].rearrange("k c a m -> k c (a m)")[:, :, 15:1024:16]

            constb = const.rearrange("k (o m) -> k o m", o=1).to_broadcast([128, KT, 64])

            def bc(a):
                return a[:, :].rearrange("k (c o) -> k c o", o=1).to_broadcast([128, KT, 64])

            def channel_means(b, p):
                dve.wait_ge(y_raw, 8 * b + 8)
                step(nc.vector.tensor_tensor(xs1[:, :, :], xcols(p), constb, ALU.mult))
                stat(b, 1)
                step(nc.vector.tensor_reduce(mc[:, :], xs1[:, :, :], AX.X, ALU.add))
                stat(b, 2)
                step(nc.vector.tensor_scalar(mc[:, :], mc[:, :], 1.0 / PIX, None, ALU.mult))
                stat(b, 3)
                step(nc.vector.tensor_tensor(xs1[:, :, :], bc(mc), constb, ALU.mult))
                stat(b, 4)
                step(nc.vector.tensor_tensor(xs1[:, :, :], xcols(p), xs1[:, :, :], ALU.subtract))
                stat(b, 5)
                step(nc.vector.tensor_tensor(xs2[:, :, :], xs1[:, :, :], xs1[:, :, :], ALU.mult))
                stat(b, 6)
                step(nc.vector.tensor_reduce(sX[:, :], xs2[:, :, :], AX.X, ALU.add))
                stat(b, 7)
                dve.wait_ge(y_sq, 4 * b + 4)
                step(nc.vector.scalar_tensor_tensor(out=sX[:, :], in0=sumsq[:, :], scalar=2.0, in1=sX[:, :], op0=ALU.mult, op1=ALU.add))

            def moments(b):
                dve.wait_ge(mean_prod, b + 1)
                step(nc.vector.tensor_copy(mg[:, :], y_bank[0][:, 0:4]))
                stat(b, 9)
                step(nc.vector.tensor_tensor(dev[:, :], mc[:, :], mg[:, :], ALU.subtract))
                stat(b, 10)
                step(nc.vector.tensor_tensor(dev[:, :], dev[:, :], dev[:, :], ALU.mult))
                stat(b, 11)
                step(nc.vector.scalar_tensor_tensor(out=qv[:, :], in0=sX[:, :], scalar=1.0 / PIX, in1=dev[:, :], op0=ALU.mult, op1=ALU.add))

            def scales(b, p):
                dve.wait_ge(var_prod, b + 1)
                step(nc.vector.tensor_scalar(var[:, :], y_bank[0][:, 8:12], GN_EPS, None, ALU.add))
                dve.wait_ge(std_ready, b + 1)
                step(nc.vector.reciprocal(rstd[:, :], std_t[:, :]))
                stat(b, 14)
                step(nc.vector.tensor_tensor(nt[:, :], rstd[:, :], rstd[:, :], ALU.mult))
                stat(b, 15)
                step(nc.vector.tensor_tensor(nt[:, :], nt[:, :], var[:, :], ALU.mult))
                stat(b, 16)
                step(nc.vector.tensor_scalar(nt[:, :], nt[:, :], -0.5, 1.5, ALU.mult, ALU.add))
                stat(b, 17)
                step(nc.vector.tensor_tensor(rstd[:, :], rstd[:, :], nt[:, :], ALU.mult))
                step(nc.vector.tensor_tensor(xs1[:, :, :], bc(mg), constb, ALU.mult))
                stat(b, 19)
                step(nc.vector.tensor_tensor(xcols(p), xcols(p), xs1[:, :, :], ALU.subtract))
                stat(b, 20)

            def normalise(b, p, ct):
                v = y[p][:, ct, :, :].rearrange("k a m -> k (a m)")
                nc.vector.tensor_scalar(v, v, rstd[:, ct:ct + 1], None, ALU.mult).then_inc(y_norm, 1)

            def image(b, p, more):
                for u in range(9):
                    rows = 96 if u in (6, 7) else 128
                    dve.wait_ge(spec_prod, 9 * b + u + 1)
                    bias = b1s[0:rows, 2 if u == 8 else u % 2, :]
                    nc.vector.tensor_tensor(r[0:rows, u, :], c_bank[u % 3][0:rows, 0:CH], bias, ALU.add).then_inc(spec_sum, 1)
                for j in range(10):
                    if j == 6 and more:
                        channel_means(b + 1, 1 - p)
                    if j == 8:
                        for half in range(2):
                            dve.wait_ge(rho_ready, 10 * b + 7 + half)
                            bs = slice(2 * half, 2 * half + 2)
                            nc.vector.tensor_copy(rhoB[0:BC, bs, :, :].rearrange("k b a m -> k (b a m)"),
                                                  rhoA[0:BC, bs, :, :].rearrange("k b a m -> k (b a m)")).then_inc(rhoB_ready, 1)
                        dve.wait_ge(rhoB_ready, 2 * b + 2)
                    dve.wait_ge(rho_prod, 10 * b + j + 1)
                    bank = b_bank[j % 3]
                    if j < 8:
                        t, half = j // 2, j % 2
                        n, nsl = (128, 4) if t < 3 else (96, 3)
                        dst = rhoA[0:BC, 2 * half:2 * half + 2, :, :].rearrange("k b a (m s t) -> k (b a m) s t", s=4, t=4)[:, :, 0:nsl, t]
                        nc.vector.tensor_copy(dst, bank[0:BC, 0:4 * n].rearrange("k (m s) -> k m s", s=nsl)).then_inc(rho_ready, 1)
                    else:
                        bs = slice(2 * (j - 8), 2 * (j - 8) + 2)
                        src = bank[0:BC, 0:264].rearrange("k (c m) -> k c m", m=66)
                        nc.vector.tensor_copy(rhoA[0:BC, bs, :, 15:512:16].rearrange("k b a m -> k (b a) m"), src[:, :, 0:32])
                        nc.vector.tensor_copy(rhoB[0:BC, bs, :, 15:512:16].rearrange("k b a m -> k (b a) m"), src[:, :, 32:64])
                        nc.vector.tensor_copy(rhoX[0:BC, bs, :, 15:32:16].rearrange("k b a m -> k (b a) m"), src[:, :, 64:66]).then_inc(rho_ready, 1)
                if more:
                    moments(b + 1)
                for q in range(4):
                    dve.wait_ge(g_prod, 8 * b + 2 * q + 2)
                    bank = c_bank[(2 * q + 1) % 3]
                    nc.vector.tensor_copy(g[64:128, 2 * q, :], bank[0:64, 0:CH]).then_inc(gi_ready, 1)
                    nc.vector.tensor_copy(g[0:64, 2 * q + 1, :], bank[64:128, 0:CH]).then_inc(gi_ready, 1)
                    if more:
                        if q == 1:
                            scales(b + 1, 1 - p)
                            normalise(b + 1, 1 - p, 0)
                            normalise(b + 1, 1 - p, 1)
                        elif q == 2:
                            normalise(b + 1, 1 - p, 2)
                            normalise(b + 1, 1 - p, 3)
                for t in range(TILES):
                    dve.wait_ge(o_prod, 8 * b + t + 1)
                    if t % 4 == 0:
                        dve.wait_ge(stored[t // 4], 16 * b + 16)
                    bank = b_bank[t % 3]
                    nc.vector.tensor_tensor(o_sb[:, t, 0:288].rearrange("p (i q) -> p i q", q=3), bank[:, 0:288].rearrange("p (i q) -> p i q", q=3),
                                            x_sb[p][:, t, :].rearrange("p (i q) -> p i q", q=4)[:, :, 0:3], ALU.add)
                    nc.vector.tensor_tensor(o_sb[:, t, 288:384], bank[:, 288:384], x_sb[p][:, t, 3:CH:4], ALU.add).then_inc(o_ready, 1)

            nc.vector.memset(y[0][96:128, 3, :, :], 0.0).then_inc(zeroed, 1)
            nc.vector.memset(y[1][96:128, 3, :, :], 0.0).then_inc(zeroed, 1)
            nc.vector.memset(rhoX[0:BC, :, :, :], 0.0).then_inc(zeroed, 1)
            nc.vector.memset(w2T[:, :, 0, BC:BC + 3], 0.0).then_inc(zeroed, 1)
            nc.vector.memset(sumsq[:, :], 0.0).then_inc(zeroed, 1)
            nc.vector.memset(rhoA[0:BC, :, :, 15:512:16], 0.0).then_inc(zeroed, 1)
            nc.vector.memset(w1R[:, :, :, :], 0.0).then_inc(zeroed, 1)
            nc.vector.memset(w2raw[96:99, :, :, :], 0.0).then_inc(zeroed, 1)
            nc.vector.memset(qv[:, :], 0.0).then_inc(o_ready, 8)
            nc.vector.memset(dev[:, :], 0.0).then_inc(gi_ready, 8)
            nc.vector.memset(mg[:, :], 0.0).then_inc(stored[0], 16)
            nc.vector.memset(nt[:, :], 0.0).then_inc(stored[1], 16)
            dve.wait_ge(consts_in, 16)
            channel_means(0, 0)
            moments(0)
            scales(0, 0)
            for ct in range(KT):
                normalise(0, 0, ct)
            dve.wait_ge(weights_in, 16 * N_WEIGHT)
            dve.wait_ge(padded_in, 16 * N_PADDED)
            nc.vector.tensor_copy(w1I[:, :, 1, :], w1R[:, :, 0, :]).then_inc(weights_ready, 1)
            nc.vector.tensor_scalar(w1I[:, :, 0, :], w1R[:, :, 1, :], -1.0, None, ALU.mult).then_inc(weights_ready, 1)
            nc.vector.tensor_copy(w2s[0:BC, :, 0, :], w2raw[0:BC, :, 0, :]).then_inc(weights_ready, 1)
            nc.vector.tensor_scalar(w2s[0:BC, :, 1, :], w2raw[0:BC, :, 1, :], -1.0, None, ALU.mult).then_inc(weights_ready, 1)
            nc.vector.tensor_scalar(w2s[BC:BC + 3, :, 0, :], w2raw[BC:BC + 3, :, 0, :], rowscale[BC:BC + 3, :], None, ALU.mult).then_inc(weights_ready, 1)
            dve.wait_ge(w2_prod, 2)
            u_bank = b_bank[0][:, 0:CH].rearrange("k (b n) -> k b n", b=BLOCKS)
            v_bank = b_bank[1][:, 0:CH].rearrange("k (b n) -> k b n", b=BLOCKS)
            nc.vector.tensor_copy(w2s[0:BC, :, 2, :], u_bank[0:BC]).then_inc(weights_ready, 1)
            nc.vector.tensor_tensor(w2s[0:BC, :, 3, :], w2raw[0:BC, :, 0, :], v_bank[0:BC], ALU.subtract).then_inc(weights_ready, 1)
            nc.vector.tensor_tensor(w2raw[BC:BC + 3, :, 1, :], w2raw[BC:BC + 3, :, 1, :], u_bank[BC:BC + 3], ALU.add).then_inc(weights_ready, 1)
            dve.wait_ge(weights_ready, 8)
            nc.vector.tensor_scalar(w2s[BC:BC + 3, :, 2, :], w2raw[BC:BC + 3, :, 1, :], rowscale[BC:BC + 3, :], None, ALU.mult).then_inc(weights_ready, 1)
            with dve.Fori(0, BATCHES - 3, 2) as b:
                for p in range(2):
                    image(b + p, p, True)
            image(BATCHES - 2, 0, True)
            image(BATCHES - 1, 1, False)


def rows_of_tiles():
    return np.array([[h for q in (2 * t, 2 * t + 1) for h in ((0, SIDE // 2) if q == 0 else (q, SIDE - q))] for t in range(TILES)])


def kernel(x, L0_conv_w1, L0_conv_b1, L0_conv_w2, L0_conv_b2, L0_conv_bias_w, L0_conv_bias_b):
    import concourse.bacc as bacc
    from concourse.bass_utils import run_bass_kernel_spmd
    rows = rows_of_tiles()
    x = np.asarray(x)
    order = np.array([[96 * ct + 3 * i + q if q < 3 else 288 + 32 * ct + i for i in range(32) for q in range(4)] for ct in range(3)]).ravel()
    xt = x[:, rows.T][..., order]
    xt = np.ascontiguousarray(xt.transpose(0, 1, 3, 2, 4)).reshape(BATCHES, 128, TILES * CH)
    w1, w2, b1, b2 = (np.asarray(a) for a in (L0_conv_w1, L0_conv_w2, L0_conv_b1, L0_conv_b2))
    tab, marks = constants()
    given = {
        "x": xt, "w1": w1, "b1": b1, "b1h": np.ascontiguousarray(b1.transpose(1, 0, 2)).reshape(2, CH),
        "w2": w2, "w2t": np.ascontiguousarray(w2.transpose(0, 1, 3, 2)), "b2": b2,
        "bias_wt": np.ascontiguousarray(np.asarray(L0_conv_bias_w).T), "bias_b": np.asarray(L0_conv_bias_b),
        "tab": tab, "marks": marks,
    }
    nc = bacc.Bacc("TRN2", target_bir_lowering=False, num_devices=1)
    arrays, args = {}, []
    for name, a in given.items():
        arrays[f"in_{name}"] = a
        args.append(nc.dram_tensor(f"in_{name}", a.shape, mybir.dt.from_np(a.dtype), kind="ExternalInput").ap())
    args.append(nc.dram_tensor("out_0", (BATCHES, 128, TILES * CH), mybir.dt.float32, kind="ExternalOutput").ap())
    spectral_block_kernel(nc, *args)
    got = run_bass_kernel_spmd(nc, [arrays], core_ids=[0]).results[0]["out_0"]
    got = got.reshape(BATCHES, 4, SIDE, TILES, CH).transpose(0, 3, 1, 2, 4)
    result = np.empty((BATCHES, SIDE, SIDE, CH), np.float32)
    result[:, rows.reshape(-1)] = got.reshape(BATCHES, SIDE, SIDE, CH)
    return result
```

```python
import numpy as np
import concourse.bass as bass
from concourse import mybir
from contextlib import ExitStack

BATCHES, SIDE, CH = 8, 32, 384
BLOCKS, BC = 4, 96
GROUP = 12
TILES = 8
KT = 4
PIX = SIDE * SIDE
GN_EPS = 1e-5
ROOT = float(np.sqrt(SIDE))


def fourier_tables():
    w = np.arange(SIDE)
    width = np.zeros((2, 4, SIDE, 2, 2, 2, 16))
    for kind in range(2):
        for j in range(2):
            first = kind == 0 and j == 0
            for kw in range(17):
                c = np.cos(2 * np.pi * kw * w / SIDE) / ROOT
                s = -np.sin(2 * np.pi * kw * w / SIDE) / ROOT
                t = width[kind, 2 * j:2 * j + 2]
                half = np.sqrt(0.5)
                if kw in (0, 16):
                    x = kw // 16
                    if first:
                        t[0, :, 0, j, x, 15] = c
                        t[1, :, 1, j, x, 15] = c
                    else:
                        t[:, :, 0, j, x, 15] = half * c
                        t[0, :, 1, j, x, 15] = -half * c
                        t[1, :, 1, j, x, 15] = half * c
                elif first:
                    for e in range(2):
                        t[e, :, 0, j, e, kw - 1] = c
                        t[e, :, 1, j, e, kw - 1] = s
                else:
                    t[:, :, 0, j, 0, kw - 1] = half * c
                    t[:, :, 1, j, 0, kw - 1] = half * s
                    for m, sign in ((0, 1), (1, -1)):
                        t[m, :, 0, j, 1, kw - 1] = sign * half * s
                        t[m, :, 1, j, 1, kw - 1] = -sign * half * c
    kh = np.arange(SIDE)
    height = np.zeros((SIDE, 16, 2))
    height[:, 0, 0] = 1
    height[:, 0, 1] = (-1.0) ** kh
    for q in range(1, 16):
        height[:, q, 0] = np.sqrt(2) * np.cos(2 * np.pi * kh * q / SIDE)
        height[:, q, 1] = np.sqrt(2) * np.sin(2 * np.pi * kh * q / SIDE)
    height /= ROOT
    hgt = np.zeros((2, TILES, 2, 2, 4, 4, SIDE))
    rows = height.reshape(SIDE, TILES, 2, 2)
    for slot in range(4):
        for kind in range(2 if slot < 3 else 1):
            hgt[kind, :, :, :, slot, slot] = rows.transpose(1, 2, 3, 0)
    xf = np.zeros((2, 2, TILES, 2, 2, 2, 2, SIDE))
    xi = np.zeros((2, 2, SIDE, 2, 66))
    xia = np.zeros((2, 2, SIDE, 2, TILES, 2, 2))
    xib = np.zeros_like(xia)
    for t in range(TILES):
        for j in range(2):
            q = 2 * t + j
            for x in range(2):
                for part in range(2):
                    xf[part, 0, t, j, x, part, x] = height[:, q, 0]
                    xia[part, x, :, part, t, j, x] = height[:, q, 0]
                    if q == 0:
                        xf[part, 1, t, j, x, part, x] = height[:, 0, 1]
                        xi[part, x, :, part, 64 + x] = height[:, 0, 1]
                    else:
                        xf[part, 1, t, j, x, 1 - part, x] = height[:, q, 1] * (1 if part == 0 else -1)
                        xib[part, x, :, part, t, j, x] = height[:, q, 1]
    xi[..., 0:32] = xia.reshape(2, 2, SIDE, 2, 32)
    xi[..., 32:64] = xib.reshape(2, 2, SIDE, 2, 32)
    back = width.copy()
    back[..., 0:15] *= 2
    width = width.reshape(2, 128, 2, 64)
    back = back.reshape(2, 128, 2, 64)
    inv = np.zeros((3, 128, 128))
    for n, (kind, odd) in enumerate(((0, 0), (1, 0), (1, 1))):
        r, i = back[kind, :, 0].T, back[kind, :, 1].T
        inv[n] = np.concatenate([i, r] if odd else [r, i])
    const = np.zeros((2, TILES, 2, 2))
    for t in range(TILES):
        got = width[0 if t == 0 else 1].sum(0).reshape(2, 2, 2, 16)[..., 15]
        const[:, t] = np.where(np.abs(got) < 1e-9, 0, got)
    return width, hgt.reshape(2, 128, 128), xf.reshape(128, 128), xi.reshape(128, 132), inv, const.reshape(64)


def group_tables():
    own = np.zeros((128, 128))
    block3 = np.zeros((BC, 4, 128))
    for a in range(128):
        for b in range(128):
            if a % 4 < 3 and b % 4 < 3 and (a // 4 * 3 + a % 4) // GROUP == (b // 4 * 3 + b % 4) // GROUP:
                own[a, b] = 1 / GROUP
    for n in range(BC):
        for m in range(BC):
            if n // GROUP == m // GROUP:
                block3[n, m // 32, 4 * (m % 32) + 3] = 1 / GROUP
                block3[n, 3, m] = 1 / GROUP
    return own, block3


Y_SCALE = 64.0
H_SCALE = 32.0
Z_EVAC = 2.0 ** -7
H_EVAC = 1 / H_SCALE
W_TOP = 8.0

TAB, TAB16 = {}, {}
TABW = TAB16W = 0
for _name, _wide in (("width", 256), ("inv", 384), ("own", 128), ("block3", 512), ("const", 64), ("rowscale", 1), ("coef", 10)):
    TAB[_name] = (TABW, TABW + _wide)
    TABW += _wide
for _name, _wide in (("height", 256), ("xf", 128), ("xi", 132), ("heightT", 256)):
    TAB16[_name] = (TAB16W, TAB16W + _wide)
    TAB16W += _wide


def constants():
    width, hgt, xf, xi, inv, const = fourier_tables()
    own, block3 = group_tables()
    tab = np.zeros((128, TABW))
    tab16 = np.zeros((128, TAB16W))

    def put(name, a):
        table, place = (tab, TAB) if name in TAB else (tab16, TAB16)
        table[:a.shape[0], place[name][0]:place[name][1]] = a.reshape(a.shape[0], -1)

    put("width", width.reshape(2, 128, 128).transpose(1, 0, 2))
    put("height", H_SCALE * hgt.transpose(1, 0, 2))
    put("xf", H_SCALE * xf)
    put("xi", H_SCALE * xi)
    put("heightT", H_SCALE * np.concatenate([hgt[0].T, hgt[1].T], axis=1))
    put("inv", inv.transpose(1, 0, 2))
    put("own", own)
    put("block3", block3)
    put("const", np.broadcast_to(const, (128, 64)))
    tab[96:99, TAB["rowscale"][0]] = [ROOT, ROOT, 8.0]
    coef = [1, 2.0 ** -8, 1, 2.0 ** -7, 2.0 ** -11]
    put("coef", np.broadcast_to(np.array([c for v in coef for c in (v, -v)]), (128, 10)))
    mark = np.zeros((3, TILES, 2, 2, 16))
    mark[0, 0, 0, 0, :] = 1
    mark[0, 0, 0, 1, 15] = 1
    mark_a = mark.copy()
    mark_a[1, 0, 0, 0, 15] = 1
    mark_a[2, :, :, 0, 15] = 1
    mark_a[2, 0, 0, 0, 15] = 0
    mark_b = mark.copy()
    mark_b[0, 0, 0, :, 15] = 0
    extra = np.zeros((3, 32))
    extra[1, 15] = 1
    marks = np.concatenate([mark_a.reshape(3, 512), mark_b.reshape(3, 512), extra], axis=1)
    tab = tab.astype(np.float32)
    high = tab16.astype(np.float16)
    low = (tab16 - high).astype(np.float16)
    return tab, np.stack([high, low], axis=1), marks.astype(np.float16)


def spectral_block_kernel(nc, x, w1, b1, b1h, w2, w2t, b2, bias_wt, bias_b, tab_d, tab16_d, marks_d, out):
    f32 = mybir.dt.float32
    f16 = mybir.dt.float16
    i32 = mybir.dt.int32
    ALU = mybir.AluOpType
    ACT = mybir.ActivationFunctionType
    AX = mybir.AxisListType
    ctx = ExitStack()
    with ctx:
        def sb(name, shape, dt=f32):
            return ctx.enter_context(nc.sbuf_tensor(name, shape, dt))

        def sem(name):
            return ctx.enter_context(nc.semaphore(name))

        x_sb = [sb(f"x_sb{p}", [128, TILES, CH]) for p in range(2)]
        o_sb = sb("o_sb", [128, TILES, CH])
        yraw = sb("yraw", [128, KT, 2, 512])
        y = [sb(f"y{p}", [128, 2, KT, 2, 512], f16) for p in range(2)]
        z = sb("z", [128, 2, 9, CH], f16)
        rsum = sb("rsum", [128, 9, CH])
        r = sb("r", [128, 2, 9, CH], f16)
        rho = sb("rho", [128, 2, BLOCKS, 2, 2, 512], f16)
        rhoX = sb("rhoX", [128, 2, BLOCKS, 2, 32], f16)
        g = sb("g", [128, TILES, CH])
        tab = sb("tab", [128, TABW])
        tab16 = sb("tab16", [128, 2, TAB16W], f16)
        w1R = sb("w1R", [128, 2, BLOCKS, 2, BC], f16)
        w1I = sb("w1I", [128, 2, BLOCKS, 2, BC], f16)
        biasw = sb("biasw", [128, 2, 3, CH], f16)
        w2s = sb("w2s", [128, 2, BLOCKS, 4, BC], f16)
        b1s = sb("b1s", [128, 3, CH])
        sumsq = sb("sumsq", [128, KT])
        mc = sb("mc", [128, KT])
        xs1 = sb("xs1", [128, KT, 64])
        xs2 = sb("xs2", [128, KT, 64])
        sX = sb("sX", [128, KT])
        mg = sb("mg", [128, KT])
        dev = sb("dev", [128, KT])
        qv = sb("qv", [128, KT])
        var = sb("var", [128, KT])
        std_t = sb("std_t", [128, KT])
        rstd = sb("rstd", [128, KT])
        nt = sb("nt", [128, KT])
        junk = sb("junk", [128, 960])
        extreme = sb("extreme", [128, 10])
        peak = sb("peak", [128, 2])
        peak_all = sb("peak_all", [128, 2])
        power = sb("power", [128, 2])
        s1 = sb("s1", [128, 1])
        s2 = sb("s2", [128, 1])
        s12h = sb("s12h", [128, 1])
        sbias = sb("sbias", [128, 1])
        unscale = sb("unscale", [128, 1])
        w2scale = sb("w2scale", [128, 1])

        def view(buf, at, rows, *dims):
            n = int(np.prod(dims))
            names = "abcd"[:len(dims)]
            flat = buf[0:rows, :, :].rearrange("k t c -> k (t c)")[:, at:at + n]
            return flat.rearrange(f"k ({' '.join(names)}) -> k {' '.join(names)}", **dict(zip(names, dims)))

        w1raw = view(o_sb, 0, 128, BLOCKS, 2, BC)
        biasraw = view(o_sb, 768, 128, 3, CH)
        w2raw = view(o_sb, 1920, 128, BLOCKS, 2, BC)
        w2f = view(g, 0, 128, BLOCKS, 4, BC)
        w2T = view(g, 1536, BC, BLOCKS, 2, BC + 3)

        banks = [ctx.enter_context(nc.psum_tensor(f"bank{i}", [128, 512], f32)) for i in range(8)]
        y_bank = banks[0:2]
        b_bank = banks[2:5]
        c_bank = banks[5:8]

        x_loaded = [[sem(f"x_loaded{p}{h}") for h in range(2)] for p in range(2)]
        consts_in = sem("consts_in")
        tables_in = sem("tables_in")
        weights_in = sem("weights_in")
        padded_in = sem("padded_in")
        zeroed = sem("zeroed")
        weights_ready = sem("weights_ready")
        w2_prod = sem("w2_prod")
        peak_ready = sem("peak_ready")
        peak_reduced = sem("peak_reduced")
        wstep = sem("wstep")
        y_prod = sem("y_prod")
        y_raw = sem("y_raw")
        y_sq = sem("y_sq")
        mean_prod = sem("mean_prod")
        var_prod = sem("var_prod")
        dve_step = sem("dve_step")
        std_ready = sem("std_ready")
        scale_ready = sem("scale_ready")
        yh_ready = sem("yh_ready")
        yl_ready = sem("yl_ready")
        z_prod = sem("z_prod")
        zh_ready = sem("zh_ready")
        zl_ready = sem("zl_ready")
        spec_prod = sem("spec_prod")
        spec_sum = sem("spec_sum")
        rh_ready = sem("rh_ready")
        rl_ready = sem("rl_ready")
        rho_prod = sem("rho_prod")
        rhoh_ready = sem("rhoh_ready")
        rhol_ready = sem("rhol_ready")
        rhoB_ready = sem("rhoB_ready")
        g_prod = sem("g_prod")
        gr_ready = sem("gr_ready")
        gi_ready = sem("gi_ready")
        o_prod = sem("o_prod")
        o_ready = sem("o_ready")
        stored = [sem(f"stored{h}") for h in range(2)]

        NSTEP = 20

        def T(name, rows=128):
            if name in TAB:
                return tab[0:rows, TAB[name][0]:TAB[name][1]]
            return tab16[0:rows, :, TAB16[name][0]:TAB16[name][1]]

        width = T("width").rearrange("k (a m) -> k a m", a=2)
        height = T("height").rearrange("k s (a m) -> k s a m", a=2)
        heightT = T("heightT").rearrange("k s (a m) -> k s a m", a=2)
        xf, xi = T("xf"), T("xi")
        inv = T("inv").rearrange("k (a m) -> k a m", a=3)
        own = T("own")
        block3 = T("block3", rows=BC).rearrange("k (a m) -> k a m", a=4)
        const = T("const")
        rowscale = T("rowscale")
        coef = T("coef")

        def weight_loads():
            for q in range(3):
                yield biasraw[q:128:4, :, :], bias_wt[0:288, :].rearrange("(b i q) n -> q i b n", q=3, b=3)[q]
            yield biasraw[3:128:4, :, :], bias_wt[288:384, :].rearrange("(b i) n -> i b n", b=3)
            for ri in range(2):
                yield w2raw[0:BC, :, ri, :], w2[ri].rearrange("b k n -> k b n")
                yield w2T[:, :, ri, 0:BC], w2t[ri].rearrange("b k n -> k b n")
            yield b1s[:, 0:2, :], b1h.rearrange("(o h) n -> o h n", o=1).to_broadcast([128, 2, CH])
            for ri in range(2):
                yield b1s[64 * ri:64 * ri + 64, 2, :], b1[ri].rearrange("(o b) n -> o (b n)", o=1).to_broadcast([64, CH])
            for blk in range(BLOCKS):
                yield rho[BC:BC + 3, 0, blk, 0, :, :].rearrange("k a m -> k (a m)"), marks_d[:, 0:1024]
                yield rhoX[BC:BC + 3, 0, blk, 0, :], marks_d[:, 1024:1056]

        def padded_loads():
            for q in range(3):
                for ri in range(2):
                    yield w1raw[q:128:4, 0:3, ri, :], w1[ri, 0:3].rearrange("b (i q) n -> q i b n", q=3)[q]
            yield w1raw[0:BC, 3, :, :], w1[:, 3, :, :].rearrange("a k n -> k a n")
            for ri in range(2):
                yield w2raw[BC:BC + 1, :, ri, :], b2[ri].rearrange("(o b) n -> o b n", o=1)
            for row in range(2):
                yield w2raw[BC + 1 + row:BC + 2 + row, :, 0, :], bias_b.rearrange("(o b n) -> o b n", o=1, b=BLOCKS)
            for blk in range(BLOCKS):
                yield w2T[:, blk, 0, BC:BC + 1], b2[0, blk, :].rearrange("(n o) -> n o", o=1)

        N_WEIGHT = len(list(weight_loads()))
        N_PADDED = len(list(padded_loads()))
        N_ZERO = 8
        N_READY = 7

        def rho_ab(s, j):
            t, half = j // 2, j % 2
            return rho[0:BC, s, 2 * half:2 * half + 2, :, :, :].rearrange("k b a x m -> k (b a) x m")[:, :, 0, t:512:4]

        def rho_x(s, j, bank):
            bs = slice(2 * (j - 8), 2 * (j - 8) + 2)
            src = bank[0:BC, 0:264].rearrange("k (c m) -> k c m", m=66)
            ab = rho[0:BC, s, bs, :, :, :].rearrange("k b a x m -> k (b a x m)")[:, 15:4096:16].rearrange("k (c m) -> k c m", m=64)
            return ab, rhoX[0:BC, s, bs, :, 15:32:16].rearrange("k b a m -> k (b a) m"), src[:, :, 0:64], src[:, :, 64:66]

        block = ctx.enter_context(nc.Block())

        @block.sync
        def _(sp):
            def load(b, p):
                for h in range(2):
                    sp.dma_start(x_sb[p][:, 4 * h:4 * h + 4, :].rearrange("p t c -> p (t c)"),
                                 x[b, :, h * 4 * CH:(h + 1) * 4 * CH]).then_inc(x_loaded[p][h], 16)

            sp.dma_start(tab[:, :], tab_d).then_inc(consts_in, 16)
            load(0, 0)
            sp.dma_start(tab16[:, :, :], tab16_d).then_inc(tables_in, 16)
            for dst, src in weight_loads():
                sp.dma_start(dst, src).then_inc(weights_in, 16)
            load(1, 1)
            sp.wait_ge(zeroed, N_ZERO)
            with nc.allow_non_contiguous_dma(reason="one column of 96 per block"):
                for dst, src in padded_loads():
                    sp.dma_start(dst, src).then_inc(padded_in, 16)

            def store(b):
                for h in range(2):
                    sp.wait_ge(o_ready, 8 * b + 8 + 4 * h + 4)
                    sp.dma_start(out[b, :, h * 4 * CH:(h + 1) * 4 * CH],
                                 o_sb[:, 4 * h:4 * h + 4, :].rearrange("p t c -> p (t c)")).then_inc(stored[h], 16)

            with sp.Fori(0, BATCHES - 3, 2) as b:
                for p in range(2):
                    store(b + p)
                    load(b + p + 2, p)
            for p in range(2):
                store(BATCHES - 2 + p)
            for h in range(2):
                sp.wait_ge(stored[h], 16 * BATCHES + 16)

        @block.tensor
        def _(pe):
            def mm(o, lhsT, rhs, start, stop, **kw):
                return nc.tensor.matmul(o, lhsT, rhs, start=start, stop=stop, **kw)

            def p1(b, p, m, first=False):
                ct, h = m // 2, m % 2
                rows = 128 if ct < 3 else BC
                if m >= 2 or not first:
                    pe.wait_ge(y_raw, 8 * b + m - 1)
                if m == 0 and not first:
                    pe.wait_ge(dve_step, NSTEP * (b - 1) + 13)
                if ct == 0:
                    pe.wait_ge(x_loaded[p][h], (b - p) * 8 + 16)
                for i in range(4):
                    t = 4 * h + i
                    src = x_sb[p][:, t, 128 * ct:128 * ct + 128] if ct < 3 else x_sb[p][:, t, 3:CH:4]
                    last = mm(y_bank[h][0:rows, 128 * i:128 * i + 128], src, width[:, 0 if t == 0 else 1, :], True, True)
                last.then_inc(y_prod, 1)

            def group_mean(src, at):
                mm(y_bank[0][:, at + 3:at + 4], block3[:, 3, :], src[0:BC, 3:4], True, True)
                mm(y_bank[0][:, at:at + 3], own, src[:, 0:3], True, False)
                for ct in range(3):
                    last = mm(y_bank[0][:, at + ct:at + ct + 1], block3[:, ct, :], src[0:BC, 3:4], False, ct == 2)
                return last

            def mean(b):
                pe.wait_ge(y_raw, 8 * b + 8)
                pe.wait_ge(dve_step, NSTEP * b + 3)
                group_mean(mc, 0).then_inc(mean_prod, 1)

            def variance(b):
                pe.wait_ge(dve_step, NSTEP * b + 12)
                group_mean(qv, 8).then_inc(var_prod, 1)

            def mm3(o, S, W, start, stop, **kw):
                mm(o, S[0], W[0], start, False, **kw)
                mm(o, S[0], W[1], False, False, **kw)
                return mm(o, S[1], W[0], False, stop, **kw)

            def c1(b, p):
                pe.wait_ge(yh_ready, 4 * b + 4)
                pe.wait_ge(yl_ready, 4 * b + 4)
                for u in range(9):
                    if u < 3:
                        pe.wait_ge(o_ready, 8 * b + (7, 8, 6)[u])
                    else:
                        pe.wait_ge(zh_ready, 9 * b + u - 2)
                        pe.wait_ge(zl_ready, 9 * b + u - 2)
                    bank = b_bank[u % 3]
                    if u < 8:
                        t, half = u // 2, u % 2
                        for k in range(2):
                            blk = 2 * half + k
                            K = 128 if blk < 3 else BC
                            o = bank[:, 192 * k:192 * k + 192]
                            for part, w in ((0, w1R), (1, w1I)):
                                S = [y[p][0:K, s, blk, part, t:512:4] for s in range(2)]
                                W = [w[0:K, s, blk, :, :].rearrange("k a n -> k (a n)") for s in range(2)]
                                last = mm3(o, S, W, part == 0, part == 1)
                    else:
                        for part in range(2):
                            for blk in range(BLOCKS):
                                K = 128 if blk < 3 else BC
                                S = [y[p][0:K, s, blk, :, :].rearrange("k a n -> k (a n)")[:, 15:1024:16] for s in range(2)]
                                W = [w1R[0:K, s, blk, part, :] for s in range(2)]
                                last = mm3(bank[64 * part:64 * part + 64, 96 * blk:96 * blk + 96], S, W, True, True)
                    last.then_inc(z_prod, 1)

            def p3(b, u):
                if u == 0:
                    pe.wait_ge(gr_ready, 8 * b + 8)
                elif u == 1:
                    pe.wait_ge(gi_ready, 8 * b + 8)
                elif u == 2:
                    pe.wait_ge(gi_ready, 8 * b + 6)
                else:
                    pe.wait_ge(spec_sum, 9 * b + u - 2)
                pe.wait_ge(zh_ready, 9 * b + u + 1)
                pe.wait_ge(zl_ready, 9 * b + u + 1)
                rows = 96 if u in (6, 7) else 128
                table = xf if u == 8 else height[:, :, u // 6, :]
                mm3(c_bank[u % 3][0:rows, 0:CH], [table[:, s, 0:rows] for s in range(2)],
                    [z[:, s, u, :] for s in range(2)], True, True).then_inc(spec_prod, 1)

            def p4(b):
                for j in range(10):
                    if j < 3:
                        pe.wait_ge(zh_ready, 9 * b + 7 + j)
                        pe.wait_ge(zl_ready, 9 * b + 7 + j)
                    else:
                        pe.wait_ge(rhoh_ready, 10 * b + j - 2)
                        pe.wait_ge(rhol_ready, 10 * b + j - 2)
                    if j < 9:
                        pe.wait_ge(rh_ready, 9 * b + j + 1)
                        pe.wait_ge(rl_ready, 9 * b + j + 1)
                    bank = b_bank[j % 3]
                    if j < 8:
                        K = 96 if j >= 6 else 128
                        for c in range(4):
                            last = mm3(bank[0:BC, 128 * c:128 * c + 128], [r[0:K, s, j, BC * c:BC * c + BC] for s in range(2)],
                                       [heightT[0:K, s, j // 6, :] for s in range(2)], True, True)
                    else:
                        for c in range(2):
                            blk = 2 * (j - 8) + c
                            last = mm3(bank[0:BC, 132 * c:132 * c + 132], [r[:, s, 8, BC * blk:BC * blk + BC] for s in range(2)],
                                       [xi[:, s, :] for s in range(2)], True, True)
                    last.then_inc(rho_prod, 1)

            def c2_bias(b, p, gi):
                q, part = gi // 2, gi % 2
                if gi < 3:
                    pe.wait_ge(spec_sum, 9 * b + 7 + gi)
                elif gi % 2:
                    pe.wait_ge(gr_ready, 8 * b + 8 + (gi - 3) + 2)
                else:
                    pe.wait_ge(gi_ready, 8 * b + 8 + (gi - 4) + 2)
                for ct in range(3):
                    mm3(c_bank[gi % 3][:, 0:CH], [y[p][:, s, ct, part, 128 * q:128 * q + 128] for s in range(2)],
                        [biasw[:, s, ct, :] for s in range(2)], ct == 0, False, skip_group_check=True)

            def c2_rho(b, gi):
                q, part = gi // 2, gi % 2
                bank = c_bank[gi % 3]
                for blk in range(BLOCKS):
                    parts = [(bank[:, BC * blk:BC * blk + BC], rho[:, :, blk, ri, part, 128 * q:128 * q + 128], ri, 2 * part + ri) for ri in range(2)]
                    if gi == 1:
                        parts += [(bank[0:32, BC * blk:BC * blk + BC], rhoX[:, :, blk, ri, :], ri, ri) for ri in range(2)]
                    for o, S, ri, w in parts:
                        K = BC + 3 if ri == 0 else BC
                        mm(o, S[0:K, 0], w2s[0:K, 0, blk, w, :], False, False, skip_group_check=True)
                        mm(o, S[0:K, 0], w2s[0:K, 1, blk, w, :], False, False, skip_group_check=True)
                        last = mm(o, S[0:BC, 1], w2s[0:BC, 0, blk, w, :], False, blk == BLOCKS - 1 and o is parts[-1][0], skip_group_check=True)
                last.then_inc(g_prod, 1)

            def p6(b):
                for t in range(TILES):
                    if t >= 3:
                        pe.wait_ge(o_ready, 8 * b + 8 + t - 2)
                    pe.wait_ge(gr_ready, 8 * b + 8 + 2 * (t // 2) + 2)
                    pe.wait_ge(gi_ready, 8 * b + 8 + 2 * (t // 2) + 2)
                    mm(b_bank[t % 3][:, 0:CH], inv[:, 0 if t == 0 else 1 + t % 2, :], g[:, t, :], True, True).then_inc(o_prod, 1)

            def image(b, p, more):
                c1(b, p)
                p3(b, 0)
                p3(b, 1)
                for m in range(8):
                    if more:
                        p1(b + 1, 1 - p, m)
                    if m < 7:
                        p3(b, m + 2)
                p4(b)
                for gi in range(3):
                    c2_bias(b, p, gi)
                pe.wait_ge(rhoh_ready, 10 * b + 10)
                pe.wait_ge(rhol_ready, 10 * b + 10)
                for gi in range(8):
                    if gi >= 3:
                        c2_bias(b, p, gi)
                    if gi == 1:
                        pe.wait_ge(rhoB_ready, 4 * b + 4)
                    c2_rho(b, gi)
                    if gi == 1 and more:
                        mean(b + 1)
                    if gi == 3 and more:
                        variance(b + 1)
                p6(b)

            pe.wait_ge(consts_in, 16)
            for m in range(8):
                p1(0, 0, m, first=True)
            pe.wait_ge(weights_in, 16 * N_WEIGHT)
            pe.wait_ge(padded_in, 16 * N_PADDED)
            for k in range(2):
                for blk in range(BLOCKS):
                    M = BC + 3 if k == 0 else BC
                    last = mm(b_bank[k][0:M, 96 * blk:96 * blk + 96], w2T[:, blk, k, 0:M], w2raw[0:BC, blk, 1, :], True, True)
                last.then_inc(w2_prod, 1)
            mean(0)
            variance(0)
            pe.wait_ge(tables_in, 16)
            pe.wait_ge(weights_ready, N_READY)
            with pe.Fori(0, BATCHES - 3, 2) as b:
                for p in range(2):
                    image(b + p, p, True)
            image(BATCHES - 2, 0, True)
            image(BATCHES - 1, 1, False)

        @block.gpsimd
        def _(pool):
            for k in range(2):
                pool.wait_ge(peak_ready, k + 1)
                nc.gpsimd.partition_all_reduce(peak_all[:, k:k + 1], peak[:, k:k + 1], 128, bass.bass_isa.ReduceOp.max).then_inc(peak_reduced, 1)

        @block.scalar
        def _(act):
            def y_copy(b, m):
                ct, h = m // 2, m % 2
                rows = 128 if ct < 3 else BC
                act.wait_ge(y_prod, 8 * b + m + 1)
                nc.scalar.activation(yraw[0:rows, ct, :, 256 * h:256 * h + 256].rearrange("k a (t m) -> k t a m", t=4),
                                     y_bank[h][0:rows, :].rearrange("k (t a m) -> k t a m", t=4, a=2), ACT.Copy).then_inc(y_raw, 1)

            def square(b, ct):
                act.wait_ge(y_raw, 8 * b + 2 * ct + 2)
                if ct:
                    act.wait_ge(y_sq, 4 * b + ct)
                nc.scalar.activation(junk[:, :].rearrange("k (a m) -> k a m", m=15),
                                     yraw[:, ct, :, :].rearrange("k a (c m) -> k (a c) m", m=16)[:, :, 0:15],
                                     ACT.Square, accum_out=sumsq[:, ct:ct + 1]).then_inc(y_sq, 1)

            def std(b):
                act.wait_ge(dve_step, NSTEP * b + 13)
                nc.scalar.activation(std_t[:, :], var[:, :], ACT.Sqrt).then_inc(std_ready, 1)

            def y_high(b, p, ct):
                act.wait_ge(dve_step, NSTEP * b + 20)
                nc.scalar.activation(y[p][:, 0, ct, :, :], yraw[:, ct, :, :], ACT.Copy, scale=rstd[:, ct:ct + 1]).then_inc(yh_ready, 1)

            def g_real(b, q):
                act.wait_ge(g_prod, 8 * b + 2 * q + 1)
                bank = c_bank[(2 * q) % 3]
                nc.scalar.activation(g[0:64, 2 * q, :], bank[0:64, 0:CH], ACT.Copy, scale=unscale[0:64, :]).then_inc(gr_ready, 1)
                nc.scalar.activation(g[64:128, 2 * q + 1, :], bank[64:128, 0:CH], ACT.Copy, scale=unscale[64:128, :]).then_inc(gr_ready, 1)

            def r_high(b, u):
                rows = 96 if u in (6, 7) else 128
                act.wait_ge(spec_sum, 9 * b + u + 1)
                nc.scalar.activation(r[0:rows, 0, u, :], rsum[0:rows, u, :], ACT.Relu).then_inc(rh_ready, 1)

            def image(b, p, more):
                for u in range(9):
                    act.wait_ge(z_prod, 9 * b + u + 1)
                    nc.scalar.activation(z[:, 0, u, :], b_bank[u % 3][:, 0:CH], ACT.Copy, scale=Z_EVAC).then_inc(zh_ready, 1)
                r_high(b, 0)
                for m in range(8):
                    if more:
                        y_copy(b + 1, m)
                    r_high(b, m + 1)
                for j in range(10):
                    act.wait_ge(rho_prod, 10 * b + j + 1)
                    bank = b_bank[j % 3]
                    if j == 8:
                        act.wait_ge(rhoh_ready, 10 * b + 8)
                        act.wait_ge(rhoB_ready, 4 * b + 4)
                    if j < 8:
                        nc.scalar.activation(rho_ab(0, j), bank[0:BC, :].rearrange("k (c m) -> k c m", m=128), ACT.Copy, scale=H_EVAC).then_inc(rhoh_ready, 1)
                    else:
                        xab, xc, src_ab, src_c = rho_x(0, j, bank)
                        nc.scalar.activation(xc, src_c, ACT.Copy, scale=H_EVAC)
                        nc.scalar.activation(xab, src_ab, ACT.Copy, scale=H_EVAC).then_inc(rhoh_ready, 1)
                if more:
                    square(b + 1, 0)
                    square(b + 1, 1)
                g_real(b, 0)
                if more:
                    square(b + 1, 2)
                    square(b + 1, 3)
                g_real(b, 1)
                if more:
                    std(b + 1)
                    y_high(b + 1, 1 - p, 0)
                    y_high(b + 1, 1 - p, 1)
                g_real(b, 2)
                if more:
                    y_high(b + 1, 1 - p, 2)
                    y_high(b + 1, 1 - p, 3)
                g_real(b, 3)

            act.wait_ge(zeroed, N_ZERO)
            nc.scalar.activation(std_t[:, :], sumsq[:, :], ACT.Copy).then_inc(gr_ready, 8)
            for m in range(8):
                y_copy(0, m)
            for ct in range(KT):
                square(0, ct)
            std(0)
            for ct in range(KT):
                y_high(0, 0, ct)
            with act.Fori(0, BATCHES - 3, 2) as b:
                for p in range(2):
                    image(b + p, p, True)
            image(BATCHES - 2, 0, True)
            image(BATCHES - 1, 1, False)

        @block.vector
        def _(dve):
            def stat(b, k):
                dve.wait_ge(dve_step, NSTEP * b + k)

            def step(ins):
                ins.then_inc(dve_step, 1)

            def xcols():
                return yraw[:, :, :, :].rearrange("k c a m -> k c (a m)")[:, :, 15:1024:16]

            constb = const.rearrange("k (o m) -> k o m", o=1).to_broadcast([128, KT, 64])

            def bc(a):
                return a[:, :].rearrange("k (c o) -> k c o", o=1).to_broadcast([128, KT, 64])

            def low(out, value, factor, high):
                return nc.vector.scalar_tensor_tensor(out=out, in0=value, scalar=factor, in1=high, op0=ALU.mult, op1=ALU.subtract)

            def channel_means(b):
                dve.wait_ge(y_raw, 8 * b + 8)
                step(nc.vector.tensor_tensor(xs1[:, :, :], xcols(), constb, ALU.mult))
                stat(b, 1)
                step(nc.vector.tensor_reduce(mc[:, :], xs1[:, :, :], AX.X, ALU.add))
                stat(b, 2)
                step(nc.vector.tensor_scalar(mc[:, :], mc[:, :], 1.0 / PIX, None, ALU.mult))
                stat(b, 3)
                step(nc.vector.tensor_tensor(xs1[:, :, :], bc(mc), constb, ALU.mult))
                stat(b, 4)
                step(nc.vector.tensor_tensor(xs1[:, :, :], xcols(), xs1[:, :, :], ALU.subtract))
                stat(b, 5)
                step(nc.vector.tensor_tensor(xs2[:, :, :], xs1[:, :, :], xs1[:, :, :], ALU.mult))
                stat(b, 6)
                step(nc.vector.tensor_reduce(sX[:, :], xs2[:, :, :], AX.X, ALU.add))

            def moments(b):
                stat(b, 7)
                dve.wait_ge(y_sq, 4 * b + 4)
                step(nc.vector.scalar_tensor_tensor(out=sX[:, :], in0=sumsq[:, :], scalar=2.0, in1=sX[:, :], op0=ALU.mult, op1=ALU.add))
                dve.wait_ge(mean_prod, b + 1)
                step(nc.vector.tensor_copy(mg[:, :], y_bank[0][:, 0:4]))
                stat(b, 9)
                step(nc.vector.tensor_tensor(dev[:, :], mc[:, :], mg[:, :], ALU.subtract))
                stat(b, 10)
                step(nc.vector.tensor_tensor(dev[:, :], dev[:, :], dev[:, :], ALU.mult))
                stat(b, 11)
                step(nc.vector.scalar_tensor_tensor(out=qv[:, :], in0=sX[:, :], scalar=1.0 / PIX, in1=dev[:, :], op0=ALU.mult, op1=ALU.add))

            def scales(b):
                dve.wait_ge(var_prod, b + 1)
                step(nc.vector.tensor_scalar(var[:, :], y_bank[0][:, 8:12], GN_EPS, None, ALU.add))
                dve.wait_ge(std_ready, b + 1)
                step(nc.vector.reciprocal(rstd[:, :], std_t[:, :]))
                stat(b, 14)
                step(nc.vector.tensor_tensor(nt[:, :], rstd[:, :], rstd[:, :], ALU.mult))
                stat(b, 15)
                step(nc.vector.tensor_tensor(nt[:, :], nt[:, :], var[:, :], ALU.mult))
                stat(b, 16)
                step(nc.vector.tensor_scalar(nt[:, :], nt[:, :], -0.5, 1.5, ALU.mult, ALU.add))
                stat(b, 17)
                step(nc.vector.scalar_tensor_tensor(out=rstd[:, :], in0=rstd[:, :], scalar=Y_SCALE, in1=nt[:, :], op0=ALU.mult, op1=ALU.mult))
                step(nc.vector.tensor_tensor(xs1[:, :, :], bc(mg), constb, ALU.mult))
                stat(b, 19)
                step(nc.vector.tensor_tensor(xcols(), xcols(), xs1[:, :, :], ALU.subtract))

            def y_low(b, p, ct):
                dve.wait_ge(dve_step, NSTEP * b + 20)
                dve.wait_ge(yh_ready, 4 * b + ct + 1)
                flat = "k a m -> k (a m)"
                low(y[p][:, 1, ct, :, :].rearrange(flat), yraw[:, ct, :, :].rearrange(flat), rstd[:, ct:ct + 1],
                    y[p][:, 0, ct, :, :].rearrange(flat)).then_inc(yl_ready, 1)

            def spectrum_sum(b, u):
                rows = 96 if u in (6, 7) else 128
                dve.wait_ge(spec_prod, 9 * b + u + 1)
                nc.vector.scalar_tensor_tensor(out=rsum[0:rows, u, :], in0=c_bank[u % 3][0:rows, 0:CH], scalar=H_EVAC,
                                               in1=b1s[0:rows, 2 if u == 8 else u % 2, :], op0=ALU.mult, op1=ALU.add).then_inc(spec_sum, 1)

            def r_low(b, u):
                rows = 96 if u in (6, 7) else 128
                dve.wait_ge(spec_sum, 9 * b + u + 1)
                dve.wait_ge(rh_ready, 9 * b + u + 1)
                nc.vector.scalar_tensor_tensor(out=r[0:rows, 1, u, :], in0=rsum[0:rows, u, :], scalar=0.0, in1=r[0:rows, 0, u, :],
                                               op0=ALU.max, op1=ALU.subtract).then_inc(rl_ready, 1)

            def copy_b(b, half):
                bs = slice(2 * half, 2 * half + 2)
                dve.wait_ge(rhoh_ready, 10 * b + 7 + half)
                dve.wait_ge(rhol_ready, 10 * b + 7 + half)
                for s in range(2):
                    v = rho[0:BC, s, bs, :, :, :].rearrange("k b a x m -> k (b a) x m")
                    nc.vector.tensor_copy(v[:, :, 1, :], v[:, :, 0, :]).then_inc(rhoB_ready, 1)

            def g_imag(b, q):
                dve.wait_ge(g_prod, 8 * b + 2 * q + 2)
                bank = c_bank[(2 * q + 1) % 3]
                nc.vector.tensor_scalar(g[64:128, 2 * q, :], bank[0:64, 0:CH], unscale[0:64, :], None, ALU.mult).then_inc(gi_ready, 1)
                nc.vector.tensor_scalar(g[0:64, 2 * q + 1, :], bank[64:128, 0:CH], unscale[64:128, :], None, ALU.mult).then_inc(gi_ready, 1)

            def image(b, p, more):
                for u in range(9):
                    dve.wait_ge(z_prod, 9 * b + u + 1)
                    dve.wait_ge(zh_ready, 9 * b + u + 1)
                    low(z[:, 1, u, :], b_bank[u % 3][:, 0:CH], Z_EVAC, z[:, 0, u, :]).then_inc(zl_ready, 1)
                spectrum_sum(b, 0)
                for u in range(1, 9):
                    spectrum_sum(b, u)
                    r_low(b, u - 1)
                r_low(b, 8)
                for j in range(10):
                    dve.wait_ge(rho_prod, 10 * b + j + 1)
                    dve.wait_ge(rhoh_ready, 10 * b + j + 1)
                    bank = b_bank[j % 3]
                    if j < 8:
                        low(rho_ab(1, j), bank[0:BC, :].rearrange("k (c m) -> k c m", m=128), H_EVAC, rho_ab(0, j)).then_inc(rhol_ready, 1)
                        if j >= 6:
                            copy_b(b, j - 6)
                    else:
                        if j == 8:
                            dve.wait_ge(rhoB_ready, 4 * b + 4)
                        xab, xc, src_ab, src_c = rho_x(1, j, bank)
                        hab, hc, _, _ = rho_x(0, j, bank)
                        low(xc, src_c, H_EVAC, hc)
                        low(xab, src_ab, H_EVAC, hab).then_inc(rhol_ready, 1)
                if more:
                    channel_means(b + 1)
                g_imag(b, 0)
                if more:
                    moments(b + 1)
                g_imag(b, 1)
                if more:
                    scales(b + 1)
                    y_low(b + 1, 1 - p, 0)
                    y_low(b + 1, 1 - p, 1)
                g_imag(b, 2)
                if more:
                    y_low(b + 1, 1 - p, 2)
                    y_low(b + 1, 1 - p, 3)
                g_imag(b, 3)
                for t in range(TILES):
                    dve.wait_ge(o_prod, 8 * b + t + 1)
                    if t % 4 == 0:
                        dve.wait_ge(stored[t // 4], 16 * b + 16)
                    bank = b_bank[t % 3]
                    nc.vector.tensor_tensor(o_sb[:, t, 0:288].rearrange("p (i q) -> p i q", q=3), bank[:, 0:288].rearrange("p (i q) -> p i q", q=3),
                                            x_sb[p][:, t, :].rearrange("p (i q) -> p i q", q=4)[:, :, 0:3], ALU.add)
                    nc.vector.tensor_tensor(o_sb[:, t, 288:384], bank[:, 288:384], x_sb[p][:, t, 3:CH:4], ALU.add).then_inc(o_ready, 1)

            zero = [yraw[96:128, 3, :, :], rhoX[0:BC, :, :, :, :], w2T[:, :, 0, BC:BC + 3], sumsq[:, :], w1raw[:, :, :, :],
                    w2raw[96:99, :, :, :], w2f[96:99, :, :, :], extreme[:, :]]
            for a in zero:
                nc.vector.memset(a, 0.0).then_inc(zeroed, 1)
            nc.vector.memset(qv[:, :], 0.0).then_inc(o_ready, 8)
            nc.vector.memset(dev[:, :], 0.0).then_inc(gi_ready, 8)
            nc.vector.memset(mg[:, :], 0.0).then_inc(stored[0], 16)
            nc.vector.memset(nt[:, :], 0.0).then_inc(stored[1], 16)

            steps = [0]

            def do(ins):
                steps[0] += 1
                ins.then_inc(wstep, 1)
                dve.wait_ge(wstep, steps[0])

            def extremes(a, col, rows=slice(0, 128)):
                for k, op in enumerate((ALU.max, ALU.min)):
                    do(nc.vector.tensor_reduce(extreme[rows, col + k:col + k + 1], a, AX.XYZ if len(a.shape) == 4 else AX.XY, op))

            def scale_of(k, out):
                dve.wait_ge(peak_reduced, k + 1)
                do(nc.vector.tensor_scalar(power[:, k:k + 1], peak_all[:, k:k + 1], 2.0 ** -60, None, ALU.max))
                bits = power[:, k:k + 1].bitcast(i32)
                do(nc.vector.tensor_scalar(bits, bits, 0x7F800000, None, ALU.bitwise_and))
                do(nc.vector.reciprocal(out, power[:, k:k + 1]))
                do(nc.vector.tensor_scalar(out, out, W_TOP, None, ALU.mult))

            def split(dst, src, scale):
                do(nc.vector.tensor_scalar(dst[0], src, scale, None, ALU.mult))
                low(dst[1], src, scale, dst[0]).then_inc(weights_ready, 1)

            dve.wait_ge(zeroed, N_ZERO)
            dve.wait_ge(consts_in, 16)
            dve.wait_ge(weights_in, 16 * N_WEIGHT)
            dve.wait_ge(padded_in, 16 * N_PADDED)
            extremes(w1raw[:, :, :, :], 0)
            extremes(b1s[:, :, :], 2)
            extremes(biasraw[:, :, :], 6)
            do(nc.vector.tensor_tensor(extreme[:, 0:4], extreme[:, 0:4], coef[:, 0:4], ALU.mult))
            do(nc.vector.tensor_reduce(peak[:, 0:1], extreme[:, 0:4], AX.X, ALU.max))
            nc.vector.tensor_copy(nt[:, 0:1], peak[:, 0:1]).then_inc(peak_ready, 1)
            channel_means(0)
            moments(0)
            scales(0)
            for ct in range(KT):
                y_low(0, 0, ct)
            do(nc.vector.tensor_copy(w2f[0:BC, :, 0, :], w2raw[0:BC, :, 0, :]))
            do(nc.vector.tensor_scalar(w2f[0:BC, :, 1, :], w2raw[0:BC, :, 1, :], -1.0, None, ALU.mult))
            do(nc.vector.tensor_scalar(w2f[BC:BC + 3, :, 0, :], w2raw[BC:BC + 3, :, 0, :], rowscale[BC:BC + 3, :], None, ALU.mult))
            dve.wait_ge(w2_prod, 2)
            u_bank = b_bank[0][:, 0:CH].rearrange("k (b n) -> k b n", b=BLOCKS)
            v_bank = b_bank[1][:, 0:CH].rearrange("k (b n) -> k b n", b=BLOCKS)
            do(nc.vector.tensor_copy(w2f[0:BC, :, 2, :], u_bank[0:BC]))
            do(nc.vector.tensor_tensor(w2f[0:BC, :, 3, :], w2raw[0:BC, :, 0, :], v_bank[0:BC], ALU.subtract))
            do(nc.vector.tensor_tensor(w2raw[BC:BC + 3, :, 1, :], w2raw[BC:BC + 3, :, 1, :], u_bank[BC:BC + 3], ALU.add))
            do(nc.vector.tensor_scalar(w2f[BC:BC + 3, :, 2, :], w2raw[BC:BC + 3, :, 1, :], rowscale[BC:BC + 3, :], None, ALU.mult))
            extremes(w2f[0:BC, :, :, :], 4, slice(0, BC))
            extremes(w2f[BC:BC + 3, :, :, :], 8, slice(BC, BC + 3))
            scale_of(0, s1[:, :])
            do(nc.vector.tensor_tensor(extreme[:, 4:10], extreme[:, 4:10], coef[:, 4:10], ALU.mult))
            do(nc.vector.tensor_scalar(extreme[:, 6:10], extreme[:, 6:10], s1[:, :], None, ALU.mult))
            do(nc.vector.tensor_reduce(peak[:, 1:2], extreme[:, 4:10], AX.X, ALU.max))
            nc.vector.tensor_copy(nt[:, 1:2], peak[:, 1:2]).then_inc(peak_ready, 1)
            split([w1R[:, s, :, :, :].rearrange("k b a n -> k (b a n)") for s in range(2)], w1raw[:, :, :, :].rearrange("k b a n -> k (b a n)"), s1[:, :])
            dve.wait_ge(weights_ready, 1)
            for s in range(2):
                nc.vector.tensor_copy(w1I[:, s, :, 1, :], w1R[:, s, :, 0, :]).then_inc(weights_ready, 1)
                nc.vector.tensor_scalar(w1I[:, s, :, 0, :], w1R[:, s, :, 1, :], -1.0, None, ALU.mult).then_inc(weights_ready, 1)
            do(nc.vector.tensor_scalar(b1s[:, :, :], b1s[:, :, :], s1[:, :], 0.5, ALU.mult, ALU.mult))
            scale_of(1, s2[:, :])
            do(nc.vector.scalar_tensor_tensor(out=s12h[:, :], in0=s1[:, :], scalar=0.5, in1=s2[:, :], op0=ALU.mult, op1=ALU.mult))
            do(nc.vector.reciprocal(unscale[:, :], s12h[:, :]))
            do(nc.vector.tensor_scalar(sbias[:, :], s12h[:, :], 1 / Y_SCALE, None, ALU.mult))
            do(nc.vector.tensor_copy(w2scale[:, :], s2[:, :]))
            do(nc.vector.tensor_copy(w2scale[96:128, :], s12h[96:128, :]))
            split([w2s[0:BC + 3, s, :, :, :].rearrange("k b a n -> k (b a n)") for s in range(2)], w2f[0:BC + 3, :, :, :].rearrange("k b a n -> k (b a n)"), w2scale[0:BC + 3, :])
            split([biasw[:, s, :, :].rearrange("k b n -> k (b n)") for s in range(2)], biasraw[:, :, :].rearrange("k b n -> k (b n)"), sbias[:, :])
            with dve.Fori(0, BATCHES - 3, 2) as b:
                for p in range(2):
                    image(b + p, p, True)
            image(BATCHES - 2, 0, True)
            image(BATCHES - 1, 1, False)


def rows_of_tiles():
    return np.array([[h for q in (2 * t, 2 * t + 1) for h in ((0, SIDE // 2) if q == 0 else (q, SIDE - q))] for t in range(TILES)])


def kernel(x, L0_conv_w1, L0_conv_b1, L0_conv_w2, L0_conv_b2, L0_conv_bias_w, L0_conv_bias_b):
    import concourse.bacc as bacc
    from concourse.bass_utils import run_bass_kernel_spmd
    rows = rows_of_tiles()
    x = np.asarray(x)
    order = np.array([[96 * ct + 3 * i + q if q < 3 else 288 + 32 * ct + i for i in range(32) for q in range(4)] for ct in range(3)]).ravel()
    xt = x[:, rows.T][..., order]
    xt = np.ascontiguousarray(xt.transpose(0, 1, 3, 2, 4)).reshape(BATCHES, 128, TILES * CH)
    w1, w2, b1, b2 = (np.asarray(a) for a in (L0_conv_w1, L0_conv_w2, L0_conv_b1, L0_conv_b2))
    tab, tab16, marks = constants()
    given = {
        "x": xt, "w1": w1, "b1": b1, "b1h": np.ascontiguousarray(b1.transpose(1, 0, 2)).reshape(2, CH),
        "w2": w2, "w2t": np.ascontiguousarray(w2.transpose(0, 1, 3, 2)), "b2": b2,
        "bias_wt": np.ascontiguousarray(np.asarray(L0_conv_bias_w).T), "bias_b": np.asarray(L0_conv_bias_b),
        "tab": tab, "tab16": tab16, "marks": marks,
    }
    nc = bacc.Bacc("TRN2", target_bir_lowering=False, num_devices=1)
    arrays, args = {}, []
    for name, a in given.items():
        arrays[f"in_{name}"] = a
        args.append(nc.dram_tensor(f"in_{name}", a.shape, mybir.dt.from_np(a.dtype), kind="ExternalInput").ap())
    args.append(nc.dram_tensor("out_0", (BATCHES, 128, TILES * CH), mybir.dt.float32, kind="ExternalOutput").ap())
    spectral_block_kernel(nc, *args)
    got = run_bass_kernel_spmd(nc, [arrays], core_ids=[0]).results[0]["out_0"]
    got = got.reshape(BATCHES, 4, SIDE, TILES, CH).transpose(0, 3, 1, 2, 4)
    result = np.empty((BATCHES, SIDE, SIDE, CH), np.float32)
    result[:, rows.reshape(-1)] = got.reshape(BATCHES, SIDE, SIDE, CH)
    return result
```

```python
import numpy as np
import concourse.bass as bass
from concourse import mybir
from contextlib import ExitStack

BATCHES, SIDE, CH = 8, 32, 384
BLOCKS, BC = 4, 96
GROUP = 12
TILES = 8
NT = 3
KT = NT + 1
PIX = SIDE * SIDE
GN_EPS = 1e-5
ROOT = float(np.sqrt(SIDE))


def fourier_tables():
    w = np.arange(SIDE)
    width = np.zeros((2, 4, SIDE, 2, 2, 2, 16))
    for kind in range(2):
        for j in range(2):
            first = kind == 0 and j == 0
            for kw in range(17):
                c = np.cos(2 * np.pi * kw * w / SIDE) / ROOT
                s = -np.sin(2 * np.pi * kw * w / SIDE) / ROOT
                t = width[kind, 2 * j:2 * j + 2]
                half = np.sqrt(0.5)
                if kw in (0, 16):
                    x = kw // 16
                    if first:
                        t[0, :, 0, j, x, 15] = c
                        t[1, :, 1, j, x, 15] = c
                    else:
                        t[:, :, 0, j, x, 15] = half * c
                        t[0, :, 1, j, x, 15] = -half * c
                        t[1, :, 1, j, x, 15] = half * c
                elif first:
                    for e in range(2):
                        t[e, :, 0, j, e, kw - 1] = c
                        t[e, :, 1, j, e, kw - 1] = s
                else:
                    t[:, :, 0, j, 0, kw - 1] = half * c
                    t[:, :, 1, j, 0, kw - 1] = half * s
                    for m, sign in ((0, 1), (1, -1)):
                        t[m, :, 0, j, 1, kw - 1] = sign * half * s
                        t[m, :, 1, j, 1, kw - 1] = -sign * half * c
    kh = np.arange(SIDE)
    height = np.zeros((SIDE, 16, 2))
    height[:, 0, 0] = 1
    height[:, 0, 1] = (-1.0) ** kh
    for q in range(1, 16):
        height[:, q, 0] = np.sqrt(2) * np.cos(2 * np.pi * kh * q / SIDE)
        height[:, q, 1] = np.sqrt(2) * np.sin(2 * np.pi * kh * q / SIDE)
    height /= ROOT
    hgt = np.zeros((2, TILES, 2, 2, 4, 4, SIDE))
    rows = height.reshape(SIDE, TILES, 2, 2)
    for slot in range(4):
        for kind in range(2 if slot < 3 else 1):
            hgt[kind, :, :, :, slot, slot] = rows.transpose(1, 2, 3, 0)
    xf = np.zeros((2, 2, TILES, 2, 2, 2, 2, SIDE))
    xi = np.zeros((2, 2, SIDE, 2, 66))
    xia = np.zeros((2, 2, SIDE, 2, TILES, 2, 2))
    xib = np.zeros_like(xia)
    for t in range(TILES):
        for j in range(2):
            q = 2 * t + j
            for x in range(2):
                for part in range(2):
                    xf[part, 0, t, j, x, part, x] = height[:, q, 0]
                    xia[part, x, :, part, t, j, x] = height[:, q, 0]
                    if q == 0:
                        xf[part, 1, t, j, x, part, x] = height[:, 0, 1]
                        xi[part, x, :, part, 64 + x] = height[:, 0, 1]
                    else:
                        xf[part, 1, t, j, x, 1 - part, x] = height[:, q, 1] * (1 if part == 0 else -1)
                        xib[part, x, :, part, t, j, x] = height[:, q, 1]
    xi[..., 0:32] = xia.reshape(2, 2, SIDE, 2, 32)
    xi[..., 32:64] = xib.reshape(2, 2, SIDE, 2, 32)
    back = width.copy()
    back[..., 0:15] *= 2
    width = width.reshape(2, 128, 2, 64)
    back = back.reshape(2, 128, 2, 64)
    inv = np.zeros((3, 128, 128))
    for n, (kind, odd) in enumerate(((0, 0), (1, 0), (1, 1))):
        r, i = back[kind, :, 0].T, back[kind, :, 1].T
        inv[n] = np.concatenate([i, r] if odd else [r, i])
    const = np.zeros((2, TILES, 2, 2))
    for t in range(TILES):
        got = width[0 if t == 0 else 1].sum(0).reshape(2, 2, 2, 16)[..., 15]
        const[:, t] = np.where(np.abs(got) < 1e-9, 0, got)
    return width, hgt.reshape(2, 128, 128), xf.reshape(128, 128), xi.reshape(128, 132), inv, const.reshape(64)


def group_tables():
    own = np.zeros((128, 128))
    block3 = np.zeros((128, 128))
    for a in range(128):
        for b in range(128):
            if a % 4 < 3 and b % 4 < 3 and (a // 4 * 3 + a % 4) // GROUP == (b // 4 * 3 + b % 4) // GROUP:
                own[a, b] = 1 / GROUP
            if a % 4 == 3 and b % 4 == 3 and a // 16 == b // 16:
                block3[a, b] = 1 / GROUP
    return own, block3


Y_SCALE = 64.0
H_SCALE = 32.0
Z_EVAC = 2.0 ** -7
H_EVAC = 1 / H_SCALE
G_EVAC = 2.0 ** -12
W_TOP = 8.0

TAB, TAB16 = {}, {}
TABW = TAB16W = 0
for _name, _wide in (("width", 256), ("own", 128), ("block3", 128), ("const", 64), ("rowscale", 1), ("coef", 5)):
    TAB[_name] = (TABW, TABW + _wide)
    TABW += _wide
for _name, _wide in (("height", 256), ("xf", 128), ("xi", 132), ("heightT", 256), ("inv", 384), ("inv_low", 384)):
    TAB16[_name] = (TAB16W, TAB16W + _wide)
    TAB16W += _wide


def constants():
    width, hgt, xf, xi, inv, const = fourier_tables()
    own, block3 = group_tables()
    tab = np.zeros((128, TABW))
    tab16 = np.zeros((128, TAB16W))

    def put(name, a):
        table, place = (tab, TAB) if name in TAB else (tab16, TAB16)
        table[:a.shape[0], place[name][0]:place[name][1]] = a.reshape(a.shape[0], -1)

    put("width", width.reshape(2, 128, 128).transpose(1, 0, 2))
    put("height", H_SCALE * hgt.transpose(1, 0, 2))
    put("xf", H_SCALE * xf)
    put("xi", H_SCALE * xi)
    put("heightT", H_SCALE * np.concatenate([hgt[0].T, hgt[1].T], axis=1))
    inv = H_SCALE * inv.transpose(1, 0, 2)
    put("inv", inv)
    put("inv_low", G_EVAC * inv.astype(np.float16))
    put("own", own)
    put("block3", block3)
    put("const", np.broadcast_to(const, (128, 64)))
    tab[96:99, TAB["rowscale"][0]] = [ROOT, ROOT, 8.0]
    put("coef", np.broadcast_to([1, 2.0 ** -8, 1, 2.0 ** -7, 2.0 ** -11], (128, 5)))
    mark = np.zeros((3, TILES, 2, 2, 16))
    mark[0, 0, 0, 0, :] = 1
    mark[0, 0, 0, 1, 15] = 1
    mark_a = mark.copy()
    mark_a[1, 0, 0, 0, 15] = 1
    mark_a[2, :, :, 0, 15] = 1
    mark_a[2, 0, 0, 0, 15] = 0
    mark_b = mark.copy()
    mark_b[0, 0, 0, :, 15] = 0
    extra = np.zeros((3, 32))
    extra[1, 15] = 1
    marks = np.concatenate([mark_a.reshape(3, 512), mark_b.reshape(3, 512), extra], axis=1)
    tab = tab.astype(np.float32)
    high = tab16.astype(np.float16)
    low = (tab16 - high).astype(np.float16)
    return tab, np.stack([high, low], axis=1), marks.astype(np.float16)


def spectral_block_kernel(nc, x, w1, b1, b1h, w2, w2t, b2, bias_wt, bias_b, tab_d, tab16_d, marks_d, out):
    f32 = mybir.dt.float32
    f16 = mybir.dt.float16
    i32 = mybir.dt.int32
    ALU = mybir.AluOpType
    ACT = mybir.ActivationFunctionType
    AX = mybir.AxisListType
    ctx = ExitStack()
    with ctx:
        def sb(name, shape, dt=f32):
            return ctx.enter_context(nc.sbuf_tensor(name, shape, dt))

        def sem(name):
            return ctx.enter_context(nc.semaphore(name))

        x_sb = [sb(f"x_sb{p}", [128, TILES, CH]) for p in range(2)]
        yraw = sb("yraw", [128, NT, 2, 512])
        y = [sb(f"y{p}", [128, 2, KT, 2, 512], f16) for p in range(2)]
        z = sb("z", [128, 2, 9, CH], f16)
        rsum = sb("rsum", [128, 9, CH])
        r = sb("r", [128, 2, 9, CH], f16)
        rho = sb("rho", [128, 2, BLOCKS, 2, 2, 512], f16)
        rhoX = sb("rhoX", [128, 2, BLOCKS, 2, 32], f16)
        g = sb("g", [128, 2, TILES, CH], f16)
        o_sb = sb("o_sb", [128, TILES, CH])
        tab = sb("tab", [128, TABW])
        tab16 = sb("tab16", [128, 2, TAB16W], f16)
        w1R = sb("w1R", [128, 2, BLOCKS, 2, BC], f16)
        w1I = sb("w1I", [128, 2, BLOCKS, 2, BC], f16)
        biasw = sb("biasw", [128, 2, 3, CH], f16)
        w2s = sb("w2s", [128, 2, BLOCKS, 4, BC], f16)
        b1s = sb("b1s", [128, 3, CH])
        sumsq = sb("sumsq", [128, NT])
        sX = sb("sX", [128, NT])
        xs1 = sb("xs1", [128, NT, 64])
        xs2 = sb("xs2", [128, NT, 64])
        mc = sb("mc", [128, NT + 1])
        mg = sb("mg", [128, NT])
        dev = sb("dev", [128, NT])
        qv = sb("qv", [128, NT + 1])
        var = sb("var", [128, NT])
        std_t = sb("std_t", [128, NT])
        rstd = sb("rstd", [128, NT])
        newton = sb("newton", [128, NT])
        junk = sb("junk", [128, 960])
        extreme = sb("extreme", [128, 5])
        b1small = sb("b1small", [2 * BLOCKS, BC])
        peaks1 = sb("peaks1", [128, 2])
        peaks2 = sb("peaks2", [128, 3])
        power = sb("power", [128, 2])
        s1 = sb("s1", [128, 1])
        s2 = sb("s2", [128, 1])
        s12h = sb("s12h", [128, 1])
        sbias = sb("sbias", [128, 1])
        w2scale = sb("w2scale", [128, 1])
        unscale = sb("unscale", [128, 1])

        def view(buf, at, rows, *dims):
            n = int(np.prod(dims))
            names = "abcd"[:len(dims)]
            flat = buf[0:rows, at:at + n]
            return flat.rearrange(f"k ({' '.join(names)}) -> k {' '.join(names)}", **dict(zip(names, dims)))

        o_words = o_sb[:, :, :].rearrange("k t c -> k (t c)")
        g_words = g[:, :, :, :].rearrange("k s t c -> k (s t c)").bitcast(f32)
        w1raw = view(o_words, 0, 128, BLOCKS, 2, BC)
        biasraw = view(o_words, 768, 128, 3, CH)
        w2raw = view(o_words, 1920, 128, BLOCKS, 2, BC)
        w2f = view(g_words, 0, 128, BLOCKS, 4, BC)
        w2T = view(g_words, 1536, BC, BLOCKS, 2, BC + 3)

        banks = [ctx.enter_context(nc.psum_tensor(f"bank{i}", [128, 512], f32)) for i in range(8)]
        y_bank = banks[0:2]
        b_bank = banks[2:5]
        c_bank = banks[5:8]

        def rho_bank(j, more):
            return (*b_bank, *(y_bank if more else c_bank[0:2]))[j % 5]

        EARLY = 3
        o_bank = [*b_bank, y_bank[1]]

        def g_halves(gi):
            low, high = slice(0, 64), slice(64, 128)
            q, part = gi // 2, gi % 2
            return (high if part else low, low, 2 * q), (low if part else high, high, 2 * q + 1)

        def g_bank(gi, more):
            return y_bank[gi] if gi < 2 and not more else c_bank[gi % 3]

        x_loaded = [[sem(f"x_loaded{p}{h}") for h in range(2)] for p in range(2)]
        width_in = sem("width_in")
        consts_in = sem("consts_in")
        tables_in = sem("tables_in")
        w1_in = sem("w1_in")
        b1_in = sem("b1_in")
        w2_in = sem("w2_in")
        bias_in = sem("bias_in")
        marks_in = sem("marks_in")
        y3_ready = sem("y3_ready")
        stored = [sem(f"stored{h}") for h in range(2)]
        w1_zeroed = sem("w1_zeroed")
        zeroed = sem("zeroed")
        w1r_ready = sem("w1r_ready")
        w1i_ready = sem("w1i_ready")
        w2_prod = sem("w2_prod")
        w2_forms = sem("w2_forms")
        w2_ready = sem("w2_ready")
        bias_ready = sem("bias_ready")
        peak_ready = sem("peak_ready")
        second_largest = sem("second_largest")
        peak_reduced = sem("peak_reduced")
        s1_ready = sem("s1_ready")
        s2_ready = sem("s2_ready")
        prep = sem("prep")
        pool_prep = sem("pool_prep")
        y_prod = sem("y_prod")
        y_raw = sem("y_raw")
        y_sq = sem("y_sq")
        dve_step = sem("dve_step")
        mean_prod = sem("mean_prod")
        var_prod = sem("var_prod")
        std_ready = sem("std_ready")
        yh_ready = sem("yh_ready")
        yl_ready = sem("yl_ready")
        z_prod, zh_ready, zl_ready = sem("z_prod"), sem("zh_ready"), sem("zl_ready")
        spec_prod = sem("spec_prod")
        spec_sum = sem("spec_sum")
        rh_ready, rl_ready = sem("rh_ready"), sem("rl_ready")
        rho_prod, rhoh_ready, rhol_ready = sem("rho_prod"), sem("rhoh_ready"), sem("rhol_ready")
        rhoB_ready = sem("rhoB_ready")
        g_prod, gh_ready, gl_ready = sem("g_prod"), sem("gh_ready"), sem("gl_ready")
        o_prod = sem("o_prod")
        o_ready = sem("o_ready")

        SHORT_UNITS = (3, 7)
        Y_ITEMS = 2 * NT
        MEANS, MOMENTS, VAR_READ, CENTRED = 4, 14, 15, 22
        NSTEP = 22

        def T(name, rows=128):
            if name in TAB:
                return tab[0:rows, TAB[name][0]:TAB[name][1]]
            return tab16[0:rows, :, TAB16[name][0]:TAB16[name][1]]

        width = T("width").rearrange("k (a m) -> k a m", a=2)
        height = T("height").rearrange("k s (a m) -> k s a m", a=2)
        heightT = T("heightT").rearrange("k s (a m) -> k s a m", a=2)
        xf, xi = T("xf"), T("xi")
        inv, inv_low = (T(name).rearrange("k s (a m) -> k s a m", a=3) for name in ("inv", "inv_low"))
        own = T("own")
        block3 = T("block3")
        const = T("const")
        rowscale = T("rowscale")
        coef = T("coef")

        def w1_loads():
            for q in range(3):
                for ri in range(2):
                    yield w1raw[q:128:4, 0:3, ri, :], w1[ri, 0:3].rearrange("b (i q) n -> q i b n", q=3)[q]
            for c in range(3):
                yield w1raw[32 * c:32 * c + 32, 3, :, :], w1[:, 3, :, :].rearrange("a (i c) n -> c i a n", c=3)[c]

        def b1_loads():
            yield b1s[:, 0:2, :], b1h.rearrange("(o h) n -> o h n", o=1).to_broadcast([128, 2, CH])
            for ri in range(2):
                yield b1s[64 * ri:64 * ri + 64, 2, :], b1[ri].rearrange("(o b) n -> o (b n)", o=1).to_broadcast([64, CH])

        def w2_loads():
            for ri in range(2):
                yield w2raw[0:BC, :, ri, :], w2[ri].rearrange("b k n -> k b n")
                yield w2T[:, :, ri, 0:BC], w2t[ri].rearrange("b k n -> k b n")
            for ri in range(2):
                yield w2raw[BC:BC + 1, :, ri, :], b2[ri].rearrange("(o b) n -> o b n", o=1)
            for row in range(2):
                yield w2raw[BC + 1 + row:BC + 2 + row, :, 0, :], bias_b.rearrange("(o b n) -> o b n", o=1, b=BLOCKS)
            for blk in range(BLOCKS):
                yield w2T[:, blk, 0, BC:BC + 1], b2[0, blk, :].rearrange("(n o) -> n o", o=1)

        def bias_loads():
            for q in range(3):
                yield biasraw[q:128:4, :, :], bias_wt[0:288, :].rearrange("(b i q) n -> q i b n", q=3, b=3)[q]
            yield biasraw[3:128:4, :, :], bias_wt[288:384, :].rearrange("(i b) n -> i b n", b=3)

        def mark_loads():
            for blk in range(BLOCKS):
                yield rho[BC:BC + 3, 0, blk, 0, :, :].rearrange("k a m -> k (a m)"), marks_d[:, 0:1024]
                yield rhoX[BC:BC + 3, 0, blk, 0, :], marks_d[:, 1024:1056]

        N_W1, N_B1, N_W2, N_BIAS, N_MARK = (len(list(loads())) for loads in (w1_loads, b1_loads, w2_loads, bias_loads, mark_loads))
        N_ZERO = 6
        WIDTH_COLS = TAB["width"][1]

        def rho_ab(s, j):
            half, t = j // 4, j % 4
            return rho[0:BC, s, 2 * half:2 * half + 2, :, :, :].rearrange("k b a x m -> k (b a) x m")[:, :, 0, t:512:4]

        def rho_blocks(s, half):
            return rho[0:BC, s, 2 * half:2 * half + 2, :, :, :].rearrange("k b a x (c p) -> k (b a) x c p", p=16)

        def block_columns(bank, blk):
            if blk < 3:
                return bank[:, 128 * blk:128 * blk + 128].rearrange("p (i q) -> p i q", q=4)[:, :, 0:3]
            return bank[:, 3:CH:4].rearrange("p (q i) -> p i q", q=3)

        def rho_x(s, j, bank):
            bs = slice(2 * (j - 8), 2 * (j - 8) + 2)
            src = bank[0:BC, 0:264].rearrange("k (c m) -> k c m", m=66)
            ab = rho[0:BC, s, bs, :, :, :].rearrange("k b a x m -> k (b a x m)")[:, 15:4096:16].rearrange("k (c m) -> k c m", m=64)
            return ab, rhoX[0:BC, s, bs, :, 15:32:16].rearrange("k b a m -> k (b a) m"), src[:, :, 0:64], src[:, :, 64:66]

        w1_parts = ([w1R[:, s, :, :, :].rearrange("k b a n -> k (b a n)") for s in range(2)], w1raw.rearrange("k b a n -> k (b a n)"), s1[:, :])
        bias_parts = ([biasw[:, s, :, :].rearrange("k b n -> k (b n)") for s in range(2)], biasraw.rearrange("k b n -> k (b n)"), sbias[:, :])
        w2_parts = ([w2s[0:BC + 3, s, :, :, :].rearrange("k b a n -> k (b a n)") for s in range(2)],
                    w2f[0:BC + 3].rearrange("k b a n -> k (b a n)"), w2scale[0:BC + 3, :])

        block = ctx.enter_context(nc.Block())

        @block.sync
        def _(sp):
            def load(b, p):
                for h in range(2):
                    sp.dma_start(x_sb[p][:, 4 * h:4 * h + 4, :].rearrange("p t c -> p (t c)"),
                                 x[b, :, h * 4 * CH:(h + 1) * 4 * CH]).then_inc(x_loaded[p][h], 16)

            sp.dma_start(tab[:, 0:WIDTH_COLS], tab_d[:, 0:WIDTH_COLS]).then_inc(width_in, 16)
            load(0, 0)
            sp.dma_start(b1small[:, :], b1.rearrange("a b n -> (a b) n")).then_inc(w1_in, 16)
            sp.wait_ge(w1_zeroed, 1)
            for dst, src in w1_loads():
                sp.dma_start(dst, src).then_inc(w1_in, 16)
            sp.dma_start(tab[:, WIDTH_COLS:TABW], tab_d[:, WIDTH_COLS:TABW]).then_inc(consts_in, 16)
            sp.wait_ge(zeroed, N_ZERO)
            with nc.allow_non_contiguous_dma(reason="one column of 96 per block"):
                for dst, src in w2_loads():
                    sp.dma_start(dst, src).then_inc(w2_in, 16)
            for dst, src in bias_loads():
                sp.dma_start(dst, src).then_inc(bias_in, 16)
            sp.dma_start(tab16[:, :, :], tab16_d).then_inc(tables_in, 16)
            for dst, src in b1_loads():
                sp.dma_start(dst, src).then_inc(b1_in, 16)
            load(1, 1)
            for dst, src in mark_loads():
                sp.dma_start(dst, src).then_inc(marks_in, 16)

            def store(b, tiles=TILES // 2):
                for t in range(0, TILES, tiles):
                    sp.wait_ge(o_ready, 8 * b + 8 + t + tiles)
                    sp.dma_start(out[b, :, t * CH:(t + tiles) * CH],
                                 o_sb[:, t:t + tiles, :].rearrange("p t c -> p (t c)")).then_inc(stored[t // 4], 16)

            def block3_rows(b, p):
                for c in range(NT):
                    sp.wait_ge(yh_ready, NT * b + c + 1)
                    sp.wait_ge(yl_ready, NT * b + c + 1)
                    sp.dma_start(y[p][32 * c:32 * c + 32, :, NT, :, :].rearrange("k s a n -> k s (a n)"),
                                 y[p][3:128:4, :, c, :, :].rearrange("k s a n -> k s (a n)")).then_inc(y3_ready, 16)

            block3_rows(0, 0)
            with sp.Fori(0, BATCHES - 3, 2) as b:
                for p in range(2):
                    block3_rows(b + p + 1, 1 - p)
                    store(b + p)
                    load(b + p + 2, p)
            block3_rows(BATCHES - 1, 1)
            store(BATCHES - 2)
            store(BATCHES - 1, tiles=1)
            for h in range(2):
                sp.wait_ge(stored[h], 16 * BATCHES + 16 * TILES // 2)

        @block.tensor
        def _(pe):
            def mm(o, lhsT, rhs, start, stop, **kw):
                return nc.tensor.matmul(o, lhsT, rhs, start=start, stop=stop, **kw)

            def p1(b, p, m, first=False):
                h, ct = m // NT, m % NT
                if m >= 2 or not first:
                    pe.wait_ge(y_raw, Y_ITEMS * b + m - 1)
                if m == 0 and not first:
                    pe.wait_ge(dve_step, NSTEP * (b - 1) + VAR_READ)
                if m == 1 and not first:
                    pe.wait_ge(o_ready, 8 * b)
                if ct == 0:
                    pe.wait_ge(x_loaded[p][h], (b - p) * 8 + 16)
                for i in range(4):
                    t = 4 * h + i
                    src = x_sb[p][:, t, 128 * ct:128 * ct + 128]
                    last = mm(y_bank[m % 2][:, 128 * i:128 * i + 128], src, width[:, 0 if t == 0 else 1, :], True, True)
                last.then_inc(y_prod, 1)

            def group_mean(src, at):
                mm(y_bank[0][:, at:at + NT], own, src[:, 0:NT], True, False)
                return mm(y_bank[0][:, at:at + NT], block3, src[:, NT:NT + 1].to_broadcast([128, NT]), False, True)

            def mean(b):
                pe.wait_ge(y_raw, Y_ITEMS * (b + 1))
                pe.wait_ge(dve_step, NSTEP * b + MEANS)
                group_mean(mc, 0).then_inc(mean_prod, 1)

            def variance(b):
                pe.wait_ge(dve_step, NSTEP * b + MOMENTS)
                group_mean(qv, 8).then_inc(var_prod, 1)

            def mm3(o, S, W, start, stop, **kw):
                mm(o, S[0], W[0], start, False, **kw)
                mm(o, S[0], W[1], False, False, **kw)
                return mm(o, S[1], W[0], False, stop, **kw)

            def c1(b, p, first):
                pe.wait_ge(yh_ready, NT * b + 2)
                pe.wait_ge(yl_ready, NT * b + 2)
                if first:
                    pe.wait_ge(w1r_ready, 2)
                    pe.wait_ge(w1i_ready, 4)
                for u in range(9):
                    if u == 4:
                        pe.wait_ge(yh_ready, NT * b + 3)
                        pe.wait_ge(yl_ready, NT * b + 3)
                        pe.wait_ge(y3_ready, 16 * NT * (b + 1))
                    if u < 3:
                        pe.wait_ge(o_ready, 8 * b + 5 + u)
                    else:
                        pe.wait_ge(zh_ready, 9 * b + u - 2)
                        pe.wait_ge(zl_ready, 9 * b + u - 2)
                    bank = b_bank[u % 3]
                    if u < 8:
                        half, t = u // 4, u % 4
                        for k in range(2):
                            blk = 2 * half + k
                            K = 128 if blk < 3 else BC
                            o = bank[:, 192 * k:192 * k + 192]
                            for part, w in ((0, w1R), (1, w1I)):
                                S = [y[p][0:K, s, blk, part, t:512:4] for s in range(2)]
                                W = [w[0:K, s, blk, :, :].rearrange("k a n -> k (a n)") for s in range(2)]
                                last = mm3(o, S, W, part == 0, part == 1)
                    else:
                        for part in range(2):
                            for blk in range(BLOCKS):
                                K = 128 if blk < 3 else BC
                                S = [y[p][0:K, s, blk, :, :].rearrange("k a n -> k (a n)")[:, 15:1024:16] for s in range(2)]
                                W = [w1R[0:K, s, blk, part, :] for s in range(2)]
                                last = mm3(bank[64 * part:64 * part + 64, 96 * blk:96 * blk + 96], S, W, True, True)
                    last.then_inc(z_prod, 1)

            def p3(b, u, first):
                if first and u == 0:
                    pe.wait_ge(tables_in, 16)
                    pe.wait_ge(w2_forms, 2)
                if u == 0:
                    pe.wait_ge(gh_ready, 16 * b + 14)
                    pe.wait_ge(gl_ready, 16 * b + 14)
                elif u == 1:
                    pe.wait_ge(gh_ready, 16 * b + 16)
                    pe.wait_ge(gl_ready, 16 * b + 16)
                elif u == 2:
                    pe.wait_ge(gh_ready, 16 * b + 12)
                    pe.wait_ge(gl_ready, 16 * b + 12)
                else:
                    pe.wait_ge(spec_sum, 9 * b + u - 2)
                pe.wait_ge(zh_ready, 9 * b + u + 1)
                pe.wait_ge(zl_ready, 9 * b + u + 1)
                rows = BC if u in SHORT_UNITS else 128
                table = xf if u == 8 else height[:, :, int(u in SHORT_UNITS), :]
                mm3(c_bank[u % 3][0:rows, 0:CH], [table[:, s, 0:rows] for s in range(2)],
                    [z[:, s, u, :] for s in range(2)], True, True).then_inc(spec_prod, 1)

            def p4(b, p, more, first):
                for j in range(10):
                    if j == 4:
                        c2_bias(b, p, 0 if more else 2, more, first)
                    if j == 3 and more:
                        pe.wait_ge(y_raw, Y_ITEMS * (b + 2))
                    elif j in (3, 4) and not more:
                        pe.wait_ge(spec_sum, 9 * b + 4 + j)
                    elif j < 3:
                        pe.wait_ge(zh_ready, 9 * b + 7 + j)
                        pe.wait_ge(zl_ready, 9 * b + 7 + j)
                    elif j > 4:
                        pe.wait_ge(rhoh_ready, 10 * b + j - 4)
                        pe.wait_ge(rhol_ready, 10 * b + j - 4)
                    if j < 9:
                        pe.wait_ge(rh_ready, 9 * b + j + 1)
                        pe.wait_ge(rl_ready, 9 * b + j + 1)
                    bank = rho_bank(j, more)
                    if j < 8:
                        K = BC if j in SHORT_UNITS else 128
                        for c in range(4):
                            last = mm3(bank[0:BC, 128 * c:128 * c + 128], [r[0:K, s, j, BC * c:BC * c + BC] for s in range(2)],
                                       [heightT[0:K, s, int(j in SHORT_UNITS), :] for s in range(2)], True, True)
                    else:
                        for c in range(2):
                            blk = 2 * (j - 8) + c
                            last = mm3(bank[0:BC, 132 * c:132 * c + 132], [r[:, s, 8, BC * blk:BC * blk + BC] for s in range(2)],
                                       [xi[:, s, :] for s in range(2)], True, True)
                    last.then_inc(rho_prod, 1)

            def c2_bias(b, p, gi, more, first, cts=range(NT)):
                if first and gi == 0:
                    pe.wait_ge(bias_ready, 2)
                q, part = gi // 2, gi % 2
                if gi < 2 and not more:
                    pass
                elif gi < 3:
                    pe.wait_ge(spec_sum, 9 * b + 7 + gi)
                else:
                    pe.wait_ge(gh_ready, 16 * b + 16 + 2 * (gi - 2))
                    pe.wait_ge(gl_ready, 16 * b + 16 + 2 * (gi - 2))
                for ct in cts:
                    mm3(g_bank(gi, more)[:, 0:CH], [y[p][:, s, ct, part, 128 * q:128 * q + 128] for s in range(2)],
                        [biasw[:, s, ct, :] for s in range(2)], ct == 0, False, skip_group_check=True)

            def c2_rho(b, gi, more, first):
                if first and gi == 0:
                    pe.wait_ge(w2_ready, 1)
                    pe.wait_ge(marks_in, 16 * N_MARK)
                q, part = gi // 2, gi % 2
                bank = g_bank(gi, more)
                for blk in range(BLOCKS):
                    columns = block_columns(bank, blk)
                    parts = [(columns, rho[:, :, blk, ri, part, 128 * q:128 * q + 128], ri, 2 * part + ri) for ri in range(2)]
                    if gi == 1:
                        parts += [(columns[0:32], rhoX[:, :, blk, ri, :], ri, ri) for ri in range(2)]
                    for o, S, ri, w in parts:
                        K = BC + 3 if ri == 0 else BC
                        mm(o, S[0:K, 0], w2s[0:K, 0, blk, w, :], False, False, skip_group_check=True)
                        mm(o, S[0:K, 0], w2s[0:K, 1, blk, w, :], False, False, skip_group_check=True)
                        last = mm(o, S[0:BC, 1], w2s[0:BC, 0, blk, w, :], False, blk == BLOCKS - 1 and o is parts[-1][0], skip_group_check=True)
                last.then_inc(g_prod, 1)

            def p6(b, tiles):
                for t in tiles:
                    if t >= 4:
                        pe.wait_ge(o_ready, 8 * b + 8 + t - 3)
                    pe.wait_ge(gh_ready, 16 * b + 16 + 4 * (t // 2) + 4)
                    pe.wait_ge(gl_ready, 16 * b + 16 + 4 * (t // 2) + 4)
                    bank, table = o_bank[t % 4][:, 0:CH], 0 if t == 0 else 1 + t % 2
                    mm(bank, inv[:, 0, table, :], g[:, 0, t, :], True, False)
                    mm(bank, inv[:, 1, table, :], g[:, 0, t, :], False, False)
                    mm(bank, inv_low[:, 0, table, :], g[:, 1, t, :], False, True).then_inc(o_prod, 1)

            def image(b, p, more=True, first=False):
                c1(b, p, first)
                p3(b, 0, first)
                p3(b, 1, first)
                for m in range(7):
                    if more and m < Y_ITEMS:
                        p1(b + 1, 1 - p, m)
                    elif not more and m in (1, 3, 5):
                        c2_bias(b, p, 0, more, first, cts=[m // 2])
                    p3(b, m + 2, first)
                p4(b, p, more, first)
                for gi in range(1, 3 if more else 2):
                    c2_bias(b, p, gi, more, first)
                pe.wait_ge(rhoh_ready, 10 * b + 10)
                pe.wait_ge(rhol_ready, 10 * b + 10)
                for gi in range(8):
                    if gi >= 3:
                        c2_bias(b, p, gi, more, first)
                    if gi == 1:
                        pe.wait_ge(rhoB_ready, 4 * b + 4)
                    if gi == 7:
                        p6(b, range(EARLY))
                    c2_rho(b, gi, more, first)
                    if gi == 1 and more:
                        mean(b + 1)
                    if gi == 3 and more:
                        variance(b + 1)
                p6(b, range(EARLY, TILES))

            pe.wait_ge(width_in, 16)
            for m in range(Y_ITEMS):
                p1(0, 0, m, first=True)
            pe.wait_ge(consts_in, 16)
            mean(0)
            variance(0)
            pe.wait_ge(w2_in, 16 * N_W2)
            for k in range(2):
                for blk in range(BLOCKS):
                    M = BC + 3 if k == 0 else BC
                    last = mm(c_bank[k][0:M, 96 * blk:96 * blk + 96], w2T[:, blk, k, 0:M], w2raw[0:BC, blk, 1, :], True, True)
                last.then_inc(w2_prod, 1)
            image(0, 0, first=True)
            with pe.Fori(1, BATCHES - 2, 2) as b:
                for p in range(2):
                    image(b + p, 1 - p)
            image(BATCHES - 1, 1, more=False)

        @block.gpsimd
        def _(pool):
            done = [0]

            def do(ins):
                done[0] += 1
                ins.then_inc(pool_prep, 1)
                pool.wait_ge(pool_prep, done[0])

            def all_peak(own, over_all):
                nc.gpsimd.partition_all_reduce(over_all, own, 128, bass.bass_isa.ReduceOp.max).then_inc(peak_reduced, 1)

            pool.wait_ge(peak_ready, 1)
            all_peak(extreme[:, 0:2], peaks1[:, :])
            pool.wait_ge(peak_reduced, 1)
            pool.wait_ge(w2_in, 16 * N_W2)
            pool.wait_ge(consts_in, 16)
            do(nc.gpsimd.tensor_copy(w2f[0:BC, :, 0, :], w2raw[0:BC, :, 0, :]))
            do(nc.gpsimd.tensor_scalar(w2f[0:BC, :, 1, :], w2raw[0:BC, :, 1, :], -1.0, None, ALU.mult))
            do(nc.gpsimd.tensor_scalar(w2f[BC:BC + 3, :, 0, :], w2raw[BC:BC + 3, :, 0, :], rowscale[BC:BC + 3, :], None, ALU.mult))
            pool.wait_ge(second_largest, 2)
            do(nc.gpsimd.tensor_copy(extreme[BC:BC + 3, 4:5], extreme[BC:BC + 3, 2:3]))
            do(nc.gpsimd.memset(extreme[BC:BC + 3, 2:3], 0.0))
            pool.wait_ge(s1_ready, 1)
            do(nc.gpsimd.tensor_tensor(extreme[:, 2:5], extreme[:, 2:5], coef[:, 2:5], ALU.mult))
            do(nc.gpsimd.tensor_scalar(extreme[:, 3:5], extreme[:, 3:5], s1[:, :], None, ALU.mult))
            all_peak(extreme[:, 2:5], peaks2[:, :])
            pool.wait_ge(peak_reduced, 2)
            pool.wait_ge(s2_ready, 1)
            (high, rest), src, scale = w2_parts
            do(nc.gpsimd.tensor_scalar(src, src, scale, None, ALU.mult))
            do(nc.gpsimd.tensor_copy(high, src))
            nc.gpsimd.tensor_tensor(rest, src, high, ALU.subtract).then_inc(w2_ready, 1)

        @block.scalar
        def _(act):
            def y_copy(b, m):
                h, ct = m // NT, m % NT
                act.wait_ge(y_prod, Y_ITEMS * b + m + 1)
                nc.scalar.activation(yraw[:, ct, :, 256 * h:256 * h + 256].rearrange("k a (t m) -> k t a m", t=4),
                                     y_bank[m % 2][:, :].rearrange("k (t a m) -> k t a m", t=4, a=2), ACT.Copy).then_inc(y_raw, 1)

            def square(b, ct):
                act.wait_ge(y_raw, Y_ITEMS * b + NT + ct + 1)
                if ct:
                    act.wait_ge(y_sq, NT * b + ct)
                nc.scalar.activation(junk[:, :].rearrange("k (a m) -> k a m", m=15),
                                     yraw[:, ct, :, :].rearrange("k a (c m) -> k (a c) m", m=16)[:, :, 0:15],
                                     ACT.Square, accum_out=sumsq[:, ct:ct + 1]).then_inc(y_sq, 1)

            def std(b):
                act.wait_ge(dve_step, NSTEP * b + VAR_READ)
                nc.scalar.activation(std_t[:, :], var[:, :], ACT.Sqrt).then_inc(std_ready, 1)

            def y_high(b, p, ct):
                act.wait_ge(dve_step, NSTEP * b + CENTRED)
                nc.scalar.activation(y[p][:, 0, ct, :, :], yraw[:, ct, :, :], ACT.Copy, scale=rstd[:, ct:ct + 1]).then_inc(yh_ready, 1)

            def g_high(b, gi, more):
                act.wait_ge(g_prod, 8 * b + gi + 1)
                for rows, src, tile in g_halves(gi):
                    nc.scalar.activation(g[rows, 0, tile, :], g_bank(gi, more)[src, 0:CH], ACT.Copy, scale=G_EVAC).then_inc(gh_ready, 1)

            def r_high(b, u):
                rows = BC if u in SHORT_UNITS else 128
                act.wait_ge(spec_sum, 9 * b + u + 1)
                nc.scalar.activation(r[0:rows, 0, u, :], rsum[0:rows, u, :], ACT.Relu).then_inc(rh_ready, 1)

            def weight_high(dst, src, scale, ready):
                nc.scalar.activation(dst[0], src, ACT.Copy, scale=scale).then_inc(ready, 1)

            def copy_b(b, half):
                act.wait_ge(rhoh_ready, 10 * b + 4 * half + 4)
                v = rho_blocks(0, half)
                nc.scalar.activation(v[:, :, 1, :, 0:15], v[:, :, 0, :, 0:15], ACT.Copy).then_inc(rhoB_ready, 1)

            def image(b, p, more=True, first=False):
                for u in range(9):
                    act.wait_ge(z_prod, 9 * b + u + 1)
                    nc.scalar.activation(z[:, 0, u, :], b_bank[u % 3][:, 0:CH], ACT.Copy, scale=Z_EVAC).then_inc(zh_ready, 1)
                r_high(b, 0)
                for m in range(8):
                    if more and m < Y_ITEMS:
                        y_copy(b + 1, m)
                    r_high(b, m + 1)
                    if first and m == 1:
                        act.wait_ge(s2_ready, 1)
                        weight_high(*bias_parts, bias_ready)
                for j in range(10):
                    if j == 4:
                        copy_b(b, 0)
                    act.wait_ge(rho_prod, 10 * b + j + 1)
                    bank = rho_bank(j, more)
                    if j == 8:
                        act.wait_ge(rhoh_ready, 10 * b + 8)
                        act.wait_ge(rhol_ready, 10 * b + 8)
                    if j < 8:
                        nc.scalar.activation(rho_ab(0, j), bank[0:BC, :].rearrange("k (c m) -> k c m", m=128), ACT.Copy, scale=H_EVAC).then_inc(rhoh_ready, 1)
                    else:
                        xab, xc, src_ab, src_c = rho_x(0, j, bank)
                        nc.scalar.activation(xc, src_c, ACT.Copy, scale=H_EVAC)
                        nc.scalar.activation(xab, src_ab, ACT.Copy, scale=H_EVAC).then_inc(rhoh_ready, 1)
                copy_b(b, 1)
                if more:
                    square(b + 1, 0)
                    square(b + 1, 1)
                g_high(b, 0, more)
                if more:
                    square(b + 1, 2)
                g_high(b, 1, more)
                g_high(b, 2, more)
                if more:
                    std(b + 1)
                g_high(b, 3, more)
                for gi in range(4, 7):
                    if more:
                        y_high(b + 1, 1 - p, gi - 4)
                    g_high(b, gi, more)
                g_high(b, 7, more)

            act.wait_ge(zeroed, N_ZERO)
            nc.scalar.activation(std_t[:, :], sumsq[:, :], ACT.Sqrt).then_inc(gh_ready, 16)
            for m in range(Y_ITEMS):
                y_copy(0, m)
            for ct in range(NT):
                square(0, ct)
            std(0)
            for s in range(2):
                act.wait_ge(w1r_ready, s + 1)
                nc.scalar.activation(w1I[:, s, :, 1, :], w1R[:, s, :, 0, :], ACT.Copy).then_inc(w1i_ready, 1)
                nc.scalar.activation(w1I[:, s, :, 0, :], w1R[:, s, :, 1, :], ACT.Copy, scale=-1.0).then_inc(w1i_ready, 1)
            for ct in range(NT):
                y_high(0, 0, ct)
            image(0, 0, first=True)
            with act.Fori(1, BATCHES - 2, 2) as b:
                for p in range(2):
                    image(b + p, 1 - p)
            image(BATCHES - 1, 1, more=False)

        @block.vector
        def _(dve):
            def stat(b, k):
                dve.wait_ge(dve_step, NSTEP * b + k)

            def step(ins):
                ins.then_inc(dve_step, 1)

            def xcols():
                return yraw[:, :, :, :].rearrange("k c a m -> k c (a m)")[:, :, 15:1024:16]

            constb = const.rearrange("k (o m) -> k o m", o=1).to_broadcast([128, NT, 64])

            def bc(a):
                return a[:, 0:NT].rearrange("k (c o) -> k c o", o=1).to_broadcast([128, NT, 64])

            def low(out, value, factor, high):
                return nc.vector.scalar_tensor_tensor(out=out, in0=value, scalar=factor, in1=high, op0=ALU.mult, op1=ALU.subtract)

            def channel_means(b):
                dve.wait_ge(y_raw, Y_ITEMS * (b + 1))
                step(nc.vector.tensor_tensor(xs1[:, :, :], xcols(), constb, ALU.mult))
                stat(b, 1)
                step(nc.vector.tensor_reduce(mc[:, 0:NT], xs1[:, :, :], AX.X, ALU.add))
                stat(b, 2)
                step(nc.vector.tensor_scalar(mc[:, 0:NT], mc[:, 0:NT], 1.0 / PIX, None, ALU.mult))
                stat(b, 3)
                step(nc.vector.tensor_reduce(mc[:, NT:NT + 1], mc[:, 0:NT], AX.X, ALU.add))
                step(nc.vector.tensor_tensor(xs1[:, :, :], bc(mc), constb, ALU.mult))
                stat(b, 5)
                step(nc.vector.tensor_tensor(xs1[:, :, :], xcols(), xs1[:, :, :], ALU.subtract))
                stat(b, 6)
                step(nc.vector.tensor_tensor(xs2[:, :, :], xs1[:, :, :], xs1[:, :, :], ALU.mult))
                stat(b, 7)
                step(nc.vector.tensor_reduce(sX[:, :], xs2[:, :, :], AX.X, ALU.add))

            def moments(b):
                stat(b, 8)
                dve.wait_ge(y_sq, NT * (b + 1))
                step(nc.vector.scalar_tensor_tensor(out=sX[:, :], in0=sumsq[:, :], scalar=2.0, in1=sX[:, :], op0=ALU.mult, op1=ALU.add))
                dve.wait_ge(mean_prod, b + 1)
                step(nc.vector.tensor_copy(mg[:, :], y_bank[0][:, 0:NT]))
                stat(b, 10)
                step(nc.vector.tensor_tensor(dev[:, :], mc[:, 0:NT], mg[:, :], ALU.subtract))
                stat(b, 11)
                step(nc.vector.tensor_tensor(dev[:, :], dev[:, :], dev[:, :], ALU.mult))
                stat(b, 12)
                step(nc.vector.scalar_tensor_tensor(out=qv[:, 0:NT], in0=sX[:, :], scalar=1.0 / PIX, in1=dev[:, :], op0=ALU.mult, op1=ALU.add))
                stat(b, 13)
                step(nc.vector.tensor_reduce(qv[:, NT:NT + 1], qv[:, 0:NT], AX.X, ALU.add))

            def scales(b):
                dve.wait_ge(var_prod, b + 1)
                step(nc.vector.tensor_scalar(var[:, :], y_bank[0][:, 8:8 + NT], GN_EPS, None, ALU.add))
                dve.wait_ge(std_ready, b + 1)
                step(nc.vector.reciprocal(rstd[:, :], std_t[:, :]))
                stat(b, 16)
                step(nc.vector.tensor_tensor(newton[:, :], rstd[:, :], rstd[:, :], ALU.mult))
                stat(b, 17)
                step(nc.vector.tensor_tensor(newton[:, :], newton[:, :], var[:, :], ALU.mult))
                stat(b, 18)
                step(nc.vector.tensor_scalar(newton[:, :], newton[:, :], -0.5, 1.5, ALU.mult, ALU.add))
                stat(b, 19)
                step(nc.vector.scalar_tensor_tensor(out=rstd[:, :], in0=rstd[:, :], scalar=Y_SCALE, in1=newton[:, :], op0=ALU.mult, op1=ALU.mult))
                step(nc.vector.tensor_tensor(xs1[:, :, :], bc(mg), constb, ALU.mult))
                stat(b, 21)
                step(nc.vector.tensor_tensor(xcols(), xcols(), xs1[:, :, :], ALU.subtract))

            def y_low(b, p, ct):
                dve.wait_ge(dve_step, NSTEP * b + CENTRED)
                dve.wait_ge(yh_ready, NT * b + ct + 1)
                flat = "k a m -> k (a m)"
                low(y[p][:, 1, ct, :, :].rearrange(flat), yraw[:, ct, :, :].rearrange(flat), rstd[:, ct:ct + 1],
                    y[p][:, 0, ct, :, :].rearrange(flat)).then_inc(yl_ready, 1)

            def spectrum_sum(b, u):
                rows = BC if u in SHORT_UNITS else 128
                dve.wait_ge(spec_prod, 9 * b + u + 1)
                nc.vector.scalar_tensor_tensor(out=rsum[0:rows, u, :], in0=c_bank[u % 3][0:rows, 0:CH], scalar=H_EVAC,
                                               in1=b1s[0:rows, u // 4, :], op0=ALU.mult, op1=ALU.add).then_inc(spec_sum, 1)

            def r_low(b, u):
                rows = BC if u in SHORT_UNITS else 128
                dve.wait_ge(spec_sum, 9 * b + u + 1)
                dve.wait_ge(rh_ready, 9 * b + u + 1)
                nc.vector.scalar_tensor_tensor(out=r[0:rows, 1, u, :], in0=rsum[0:rows, u, :], scalar=0.0, in1=r[0:rows, 0, u, :],
                                               op0=ALU.max, op1=ALU.subtract).then_inc(rl_ready, 1)

            def copy_b(b, half):
                dve.wait_ge(rhol_ready, 10 * b + 4 * half + 4)
                v = rho_blocks(1, half)
                nc.vector.tensor_copy(v[:, :, 1, :, 0:15], v[:, :, 0, :, 0:15]).then_inc(rhoB_ready, 1)

            def g_low(b, gi, more):
                dve.wait_ge(g_prod, 8 * b + gi + 1)
                for n, (rows, src, tile) in enumerate(g_halves(gi)):
                    dve.wait_ge(gh_ready, 16 * b + 16 + 2 * gi + n + 1)
                    nc.vector.scalar_tensor_tensor(out=g[rows, 1, tile, :], in0=g[rows, 0, tile, :], scalar=-1 / G_EVAC, in1=g_bank(gi, more)[src, 0:CH],
                                                   op0=ALU.mult, op1=ALU.add).then_inc(gl_ready, 1)

            def add_x(b, p, t):
                dve.wait_ge(o_prod, 8 * b + t + 1)
                if t % 4 == 0:
                    dve.wait_ge(stored[t // 4], 16 * b + 16)
                nc.vector.scalar_tensor_tensor(out=o_sb[:, t, :], in0=o_bank[t % 4][:, 0:CH], scalar=unscale[:, :], in1=x_sb[p][:, t, :],
                                               op0=ALU.mult, op1=ALU.add).then_inc(o_ready, 1)

            def image(b, p, more=True, first=False):
                for u in range(9):
                    dve.wait_ge(z_prod, 9 * b + u + 1)
                    dve.wait_ge(zh_ready, 9 * b + u + 1)
                    low(z[:, 1, u, :], b_bank[u % 3][:, 0:CH], Z_EVAC, z[:, 0, u, :]).then_inc(zl_ready, 1)
                    if first and u == 1:
                        largest_weight()
                    if first and u == 5:
                        second_scales()
                if first:
                    scale_b1()
                spectrum_sum(b, 0)
                for u in range(1, 9):
                    spectrum_sum(b, u)
                    r_low(b, u - 1)
                    if first and u == 3:
                        weight_low(*bias_parts, bias_ready)
                r_low(b, 8)
                for j in range(10):
                    if j == 4:
                        copy_b(b, 0)
                    dve.wait_ge(rho_prod, 10 * b + j + 1)
                    dve.wait_ge(rhoh_ready, 10 * b + j + 1)
                    bank = rho_bank(j, more)
                    if j < 8:
                        low(rho_ab(1, j), bank[0:BC, :].rearrange("k (c m) -> k c m", m=128), H_EVAC, rho_ab(0, j)).then_inc(rhol_ready, 1)
                    else:
                        if j == 8:
                            dve.wait_ge(rhol_ready, 10 * b + 8)
                        xab, xc, src_ab, src_c = rho_x(1, j, bank)
                        hab, hc, _, _ = rho_x(0, j, bank)
                        low(xc, src_c, H_EVAC, hc)
                        low(xab, src_ab, H_EVAC, hab).then_inc(rhol_ready, 1)
                copy_b(b, 1)
                if more:
                    channel_means(b + 1)
                g_low(b, 0, more)
                if more:
                    moments(b + 1)
                g_low(b, 1, more)
                g_low(b, 2, more)
                if more:
                    scales(b + 1)
                g_low(b, 3, more)
                for gi in range(4, 7):
                    if more:
                        y_low(b + 1, 1 - p, gi - 4)
                    g_low(b, gi, more)
                for t in range(EARLY):
                    add_x(b, p, t)
                g_low(b, 7, more)
                for t in range(EARLY, TILES):
                    add_x(b, p, t)

            nc.vector.memset(w1raw[:, :, :, :], 0.0).then_inc(w1_zeroed, 1)
            for a in (w2T[:, :, 0, BC:BC + 3], w2raw[96:99, :, :, :], w2f[96:99, :, :, :], rhoX[0:BC, :, :, :, :],
                      extreme[:, :], sumsq[:, :]):
                nc.vector.memset(a, 0.0).then_inc(zeroed, 1)
            nc.vector.memset(qv[:, :], 0.0).then_inc(o_ready, 8)
            nc.vector.memset(dev[:, :], 0.0).then_inc(gl_ready, 16)
            nc.vector.memset(mg[:, :], 0.0).then_inc(stored[0], 16)
            nc.vector.memset(newton[:, :], 0.0).then_inc(stored[1], 16)

            steps = [0]

            def do(ins):
                steps[0] += 1
                ins.then_inc(prep, 1)
                dve.wait_ge(prep, steps[0])

            def scale_of(k, peaks, out):
                dve.wait_ge(peak_reduced, k + 1)
                do(nc.vector.tensor_reduce(power[:, k:k + 1], peaks, AX.X, ALU.max))
                do(nc.vector.tensor_scalar(power[:, k:k + 1], power[:, k:k + 1], 2.0 ** -60, None, ALU.max))
                bits = power[:, k:k + 1].bitcast(i32)
                do(nc.vector.tensor_scalar(bits, bits, 0x7F800000, None, ALU.bitwise_and))
                do(nc.vector.reciprocal(out, power[:, k:k + 1]))
                do(nc.vector.tensor_scalar(out, out, W_TOP, None, ALU.mult))

            def first_scale():
                dve.wait_ge(zeroed, N_ZERO)
                dve.wait_ge(consts_in, 16)
                dve.wait_ge(w1_in, 16 * (N_W1 + 1))
                do(nc.vector.tensor_reduce(extreme[:, 0:1], w1raw[:, :, :, :], AX.XYZ, ALU.max, apply_absolute_value=True))
                do(nc.vector.tensor_reduce(extreme[0:2 * BLOCKS, 1:2], b1small[:, :], AX.X, ALU.max, apply_absolute_value=True))
                nc.vector.tensor_tensor(extreme[:, 0:2], extreme[:, 0:2], coef[:, 0:2], ALU.mult).then_inc(peak_ready, 1)
                scale_of(0, peaks1[:, :], s1[:, :])
                nc.vector.tensor_copy(newton[:, 1:2], s1[:, :]).then_inc(s1_ready, 1)

            def scale_b1():
                dve.wait_ge(b1_in, 16 * N_B1)
                do(nc.vector.tensor_scalar(b1s[:, :, :], b1s[:, :, :], s1[:, :], 0.5, ALU.mult, ALU.mult))

            def weight_low(dst, src, scale, ready):
                dve.wait_ge(ready, 1)
                low(dst[1], src, scale, dst[0]).then_inc(ready, 1)

            def second_forms():
                dve.wait_ge(w2_prod, 2)
                dve.wait_ge(pool_prep, 3)
                u_bank = c_bank[0][:, 0:CH].rearrange("k (b n) -> k b n", b=BLOCKS)
                v_bank = c_bank[1][:, 0:CH].rearrange("k (b n) -> k b n", b=BLOCKS)
                do(nc.vector.tensor_copy(w2f[0:BC, :, 2, :], u_bank[0:BC]))
                do(nc.vector.tensor_tensor(w2raw[BC:BC + 3, :, 1, :], w2raw[BC:BC + 3, :, 1, :], u_bank[BC:BC + 3], ALU.add))
                nc.vector.tensor_tensor(w2f[0:BC, :, 3, :], w2raw[0:BC, :, 0, :], v_bank[0:BC], ALU.subtract).then_inc(w2_forms, 1)
                nc.vector.tensor_scalar(w2f[BC:BC + 3, :, 2, :], w2raw[BC:BC + 3, :, 1, :], rowscale[BC:BC + 3, :], None, ALU.mult).then_inc(w2_forms, 1)

            def largest_weight():
                dve.wait_ge(w2_forms, 2)
                nc.vector.tensor_reduce(extreme[0:BC + 3, 2:3], w2f[0:BC + 3, :, :, :], AX.XYZ, ALU.max, apply_absolute_value=True).then_inc(second_largest, 1)

            def largest_bias():
                dve.wait_ge(bias_in, 16 * N_BIAS)
                nc.vector.tensor_reduce(extreme[:, 3:4], biasraw[:, :, :], AX.XY, ALU.max, apply_absolute_value=True).then_inc(second_largest, 1)

            def second_scales():
                scale_of(1, peaks2[:, :], s2[:, :])
                do(nc.vector.scalar_tensor_tensor(out=s12h[:, :], in0=s1[:, :], scalar=0.5, in1=s2[:, :], op0=ALU.mult, op1=ALU.mult))
                do(nc.vector.tensor_scalar(sbias[:, :], s12h[:, :], 1 / Y_SCALE, None, ALU.mult))
                do(nc.vector.tensor_copy(w2scale[:, :], s2[:, :]))
                do(nc.vector.tensor_copy(w2scale[96:128, :], s12h[96:128, :]))
                do(nc.vector.reciprocal(unscale[:, :], s12h[:, :]))
                nc.vector.tensor_scalar(unscale[:, :], unscale[:, :], 1 / (G_EVAC * H_SCALE), None, ALU.mult).then_inc(s2_ready, 1)

            first_scale()
            channel_means(0)
            (w1_high, _), w1_src, w1_scale = w1_parts
            nc.vector.tensor_scalar(w1_high, w1_src, w1_scale, None, ALU.mult).then_inc(w1r_ready, 1)
            moments(0)
            weight_low(*w1_parts, w1r_ready)
            scales(0)
            for ct in range(NT):
                y_low(0, 0, ct)
            largest_bias()
            second_forms()
            image(0, 0, first=True)
            with dve.Fori(1, BATCHES - 2, 2) as b:
                for p in range(2):
                    image(b + p, 1 - p)
            image(BATCHES - 1, 1, more=False)


def rows_of_tiles():
    return np.array([[h for q in (2 * t, 2 * t + 1) for h in ((0, SIDE // 2) if q == 0 else (q, SIDE - q))] for t in range(TILES)])


def kernel(x, L0_conv_w1, L0_conv_b1, L0_conv_w2, L0_conv_b2, L0_conv_bias_w, L0_conv_bias_b):
    import concourse.bacc as bacc
    from concourse.bass_utils import run_bass_kernel_spmd
    rows = rows_of_tiles()
    x = np.asarray(x)
    order = np.array([[96 * ct + 3 * i + q if q < 3 else 288 + 3 * i + ct for i in range(32) for q in range(4)] for ct in range(3)]).ravel()
    xt = x[:, rows.T][..., order]
    xt = np.ascontiguousarray(xt.transpose(0, 1, 3, 2, 4)).reshape(BATCHES, 128, TILES * CH)
    w1, w2, b1, b2 = (np.asarray(a) for a in (L0_conv_w1, L0_conv_w2, L0_conv_b1, L0_conv_b2))
    tab, tab16, marks = constants()
    given = {
        "x": xt, "w1": w1, "b1": b1, "b1h": np.ascontiguousarray(b1.transpose(1, 0, 2)).reshape(2, CH),
        "w2": w2, "w2t": np.ascontiguousarray(w2.transpose(0, 1, 3, 2)), "b2": b2,
        "bias_wt": np.ascontiguousarray(np.asarray(L0_conv_bias_w).T[:, order]), "bias_b": np.asarray(L0_conv_bias_b),
        "tab": tab, "tab16": tab16, "marks": marks,
    }
    nc = bacc.Bacc("TRN2", target_bir_lowering=False, num_devices=1)
    arrays, args = {}, []
    for name, a in given.items():
        arrays[f"in_{name}"] = a
        args.append(nc.dram_tensor(f"in_{name}", a.shape, mybir.dt.from_np(a.dtype), kind="ExternalInput").ap())
    args.append(nc.dram_tensor("out_0", (BATCHES, 128, TILES * CH), mybir.dt.float32, kind="ExternalOutput").ap())
    spectral_block_kernel(nc, *args)
    got = run_bass_kernel_spmd(nc, [arrays], core_ids=[0]).results[0]["out_0"]
    got = got.reshape(BATCHES, 4, SIDE, TILES, CH).transpose(0, 3, 1, 2, 4)
    result = np.empty((BATCHES, SIDE, SIDE, CH), np.float32)
    natural = np.empty((BATCHES, SIDE, SIDE, CH), np.float32)
    natural[..., order] = got.reshape(BATCHES, SIDE, SIDE, CH)
    result[:, rows.reshape(-1)] = natural
    return result
```
